# Optimizing a Trainium2 kernel written in Bass

```python
import numpy as np
import jax
import jax.numpy as jnp

def _softmax(x, axis=-1):
    return jax.nn.softmax(x, axis=axis)

def _gelu(x):
    return jax.nn.gelu(x, approximate=True)

def _silu(x):
    return jax.nn.silu(x)

def _sigmoid(x):
    return jax.nn.sigmoid(x)

def _layernorm(x, axis=-1, eps=1e-05):
    m = jnp.mean(x, axis=axis, keepdims=True)
    v = jnp.var(x, axis=axis, keepdims=True)
    return (x - m) / jnp.sqrt(v + eps)

def _scatter_add(tgt, idx, src, axis=0):
    return tgt.at[idx].add(src)

def _segment_sum(src, seg, n):
    return jax.ops.segment_sum(src, seg, n)
kernel_name = 'mk_cond_seq_d2_seqx_r4_830f2a'

def setup_inputs(seed: int=0):
    np.random.seed(seed)
    _w = jnp.asarray

    def _rec_inputs():
        import jax
        import jax.numpy as jnp
        _rk = jax.random.key(seed)
        x = 7.22e-05 + 1 * jax.random.normal(jax.random.fold_in(_rk, 1), (8, 512, 256), jnp.float32)
        _lenS = 512 - jax.random.randint(jax.random.fold_in(_rk, 7), (8,), 0, max(1, 512 // 4) + 1, jnp.int32)
        _lenS2 = 512 - jax.random.randint(jax.random.fold_in(_rk, 8), (8,), 0, max(1, 512 // 4) + 1, jnp.int32)
        cond_256 = -0.0209273 + 1.04763 * jax.random.normal(jax.random.fold_in(_rk, 11), (8, 64), jnp.float32)
        return (x, cond_256)
    x, cond_256 = _rec_inputs()

    def _L0_cond_setup():
        import jax, jax.numpy as jnp
        import numpy as np
        from math import sqrt
        D_MODEL = 256
        N_HEADS = 16
        D_T = 64
        D_HID = 4 * D_MODEL
        EPS = 1e-06

        def _rmsnorm(x):
            return x * jax.lax.rsqrt(jnp.mean(x * x, axis=-1, keepdims=True) + EPS)

        def _ada_rmsnorm(x, t, gamma_w, beta_w):
            gamma = (t @ gamma_w.T)[:, None, :]
            beta = (t @ beta_w.T)[:, None, :]
            return gamma * _rmsnorm(x) + beta

        def _attention(x, W_q, W_k, W_v, W_o):
            b, l, dm = x.shape
            d_head = dm // N_HEADS
            scale = sqrt(N_HEADS / dm)

            def split(y):
                return y.reshape(b, l, N_HEADS, d_head).transpose(0, 2, 1, 3)
            q = split(x @ W_q.T)
            k = split(x @ W_k.T)
            v = split(x @ W_v.T)
            attn = jax.nn.softmax(scale * jnp.einsum('bnqd,bnkd->bnqk', q, k), axis=-1)
            o = jnp.einsum('bnqk,bnkd->bnqd', attn, v)
            o = o.transpose(0, 2, 1, 3).reshape(b, l, dm)
            return o @ W_o.T

        def _swiglu(x, gate_w, hidden_w, out_w, out_b):
            return jax.nn.silu(x @ gate_w.T) * (x @ hidden_w.T) @ out_w.T + out_b
        key = jax.random.key(seed)
        ks = jax.random.split(key, 16)
        s = 0.02
        inp = {'x': jax.random.normal(ks[0], (4, 512, D_MODEL), dtype=jnp.float32), 't': jax.random.normal(ks[1], (4, D_T), dtype=jnp.float32), 'attn_gamma_w': jax.random.normal(ks[2], (D_MODEL, D_T), dtype=jnp.float32) * s, 'attn_beta_w': jax.random.normal(ks[3], (D_MODEL, D_T), dtype=jnp.float32) * s, 'W_q': jax.random.normal(ks[4], (D_MODEL, D_MODEL), dtype=jnp.float32) * s, 'W_k': jax.random.normal(ks[5], (D_MODEL, D_MODEL), dtype=jnp.float32) * s, 'W_v': jax.random.normal(ks[6], (D_MODEL, D_MODEL), dtype=jnp.float32) * s, 'W_o': jax.random.normal(ks[7], (D_MODEL, D_MODEL), dtype=jnp.float32) * s, 'attn_alpha_w': jax.random.normal(ks[8], (D_MODEL, D_T), dtype=jnp.float32) * s, 'ffn_gamma_w': jax.random.normal(ks[9], (D_MODEL, D_T), dtype=jnp.float32) * s, 'ffn_beta_w': jax.random.normal(ks[10], (D_MODEL, D_T), dtype=jnp.float32) * s, 'gate_w': jax.random.normal(ks[11], (D_HID, D_MODEL), dtype=jnp.float32) * s, 'hidden_w': jax.random.normal(ks[12], (D_HID, D_MODEL), dtype=jnp.float32) * s, 'out_w': jax.random.normal(ks[13], (D_MODEL, D_HID), dtype=jnp.float32) * s, 'out_b': jnp.zeros((D_MODEL,), dtype=jnp.float32), 'ffn_alpha_w': jax.random.normal(ks[14], (D_MODEL, D_T), dtype=jnp.float32) * s}
        return inp
    _L0_cond_all = _L0_cond_setup()
    _L0_cond_in = {k: v for k, v in _L0_cond_all.items() if k in ('attn_gamma_w', 'attn_beta_w', 'W_q', 'W_k', 'W_v', 'W_o', 'attn_alpha_w', 'ffn_gamma_w', 'ffn_beta_w', 'gate_w', 'hidden_w', 'out_w', 'out_b', 'ffn_alpha_w')}
    del _L0_cond_all

    def _L1_cond_setup():
        import jax, jax.numpy as jnp
        import numpy as np
        EPS = 1e-06

        def act_quant(x):
            scale = 127.0 / jnp.clip(jnp.max(jnp.abs(x), axis=-1, keepdims=True), 1e-05, None)
            return jnp.clip(jnp.round(x * scale), -128.0, 127.0) / scale

        def weight_quant(w):
            scale = 1.0 / jnp.clip(jnp.mean(jnp.abs(w)), 1e-05, None)
            return jnp.clip(jnp.round(w * scale), -1.0, 1.0) / scale
        key = jax.random.key(seed)
        k0, k1, k2, k3, k4 = jax.random.split(key, 5)
        B, S, D, FF, C = (4, 1024, 256, 1024, 64)
        return {'x': jax.random.normal(k0, (B, S, D), jnp.float32), 'cond': jax.random.normal(k1, (B, C), jnp.float32), 'norm_w': jax.random.normal(k2, (D, C), jnp.float32) * 0.02, 'up_w': jax.random.normal(k3, (2 * FF, D), jnp.float32) * 0.02, 'down_w': jax.random.normal(k4, (D, FF), jnp.float32) * 0.02}
    _L1_cond_all = _L1_cond_setup()
    _L1_cond_in = {k: v for k, v in _L1_cond_all.items() if k in ('norm_w', 'up_w', 'down_w')}
    del _L1_cond_all
    return {'x': x, 'cond_256': cond_256, 'L0_cond_attn_gamma_w': _L0_cond_in['attn_gamma_w'], 'L0_cond_attn_beta_w': _L0_cond_in['attn_beta_w'], 'L0_cond_W_q': _L0_cond_in['W_q'], 'L0_cond_W_k': _L0_cond_in['W_k'], 'L0_cond_W_v': _L0_cond_in['W_v'], 'L0_cond_W_o': _L0_cond_in['W_o'], 'L0_cond_attn_alpha_w': _L0_cond_in['attn_alpha_w'], 'L0_cond_ffn_gamma_w': _L0_cond_in['ffn_gamma_w'], 'L0_cond_ffn_beta_w': _L0_cond_in['ffn_beta_w'], 'L0_cond_gate_w': _L0_cond_in['gate_w'], 'L0_cond_hidden_w': _L0_cond_in['hidden_w'], 'L0_cond_out_w': _L0_cond_in['out_w'], 'L0_cond_out_b': _L0_cond_in['out_b'], 'L0_cond_ffn_alpha_w': _L0_cond_in['ffn_alpha_w'], 'L1_cond_norm_w': _L1_cond_in['norm_w'], 'L1_cond_up_w': _L1_cond_in['up_w'], 'L1_cond_down_w': _L1_cond_in['down_w']}

def reference(x, cond_256, L0_cond_attn_gamma_w, L0_cond_attn_beta_w, L0_cond_W_q, L0_cond_W_k, L0_cond_W_v, L0_cond_W_o, L0_cond_attn_alpha_w, L0_cond_ffn_gamma_w, L0_cond_ffn_beta_w, L0_cond_gate_w, L0_cond_hidden_w, L0_cond_out_w, L0_cond_out_b, L0_cond_ffn_alpha_w, L1_cond_norm_w, L1_cond_up_w, L1_cond_down_w):
    import jax
    import jax.numpy as jnp

    def _L0_cond_ref(x, t, attn_gamma_w, attn_beta_w, W_q, W_k, W_v, W_o, attn_alpha_w, ffn_gamma_w, ffn_beta_w, gate_w, hidden_w, out_w, out_b, ffn_alpha_w):
        import jax, jax.numpy as jnp
        import numpy as np
        from math import sqrt
        D_MODEL = 256
        N_HEADS = 16
        D_T = 64
        D_HID = 4 * D_MODEL
        EPS = 1e-06

        def _rmsnorm(x):
            return x * jax.lax.rsqrt(jnp.mean(x * x, axis=-1, keepdims=True) + EPS)

        def _ada_rmsnorm(x, t, gamma_w, beta_w):
            gamma = (t @ gamma_w.T)[:, None, :]
            beta = (t @ beta_w.T)[:, None, :]
            return gamma * _rmsnorm(x) + beta

        def _attention(x, W_q, W_k, W_v, W_o):
            b, l, dm = x.shape
            d_head = dm // N_HEADS
            scale = sqrt(N_HEADS / dm)

            def split(y):
                return y.reshape(b, l, N_HEADS, d_head).transpose(0, 2, 1, 3)
            q = split(x @ W_q.T)
            k = split(x @ W_k.T)
            v = split(x @ W_v.T)
            attn = jax.nn.softmax(scale * jnp.einsum('bnqd,bnkd->bnqk', q, k), axis=-1)
            o = jnp.einsum('bnqk,bnkd->bnqd', attn, v)
            o = o.transpose(0, 2, 1, 3).reshape(b, l, dm)
            return o @ W_o.T

        def _swiglu(x, gate_w, hidden_w, out_w, out_b):
            return jax.nn.silu(x @ gate_w.T) * (x @ hidden_w.T) @ out_w.T + out_b
        a_alpha = (t @ attn_alpha_w.T)[:, None, :]
        x = x + a_alpha * _attention(_ada_rmsnorm(x, t, attn_gamma_w, attn_beta_w), W_q, W_k, W_v, W_o)
        f_alpha = (t @ ffn_alpha_w.T)[:, None, :]
        return x + f_alpha * _swiglu(_ada_rmsnorm(x, t, ffn_gamma_w, ffn_beta_w), gate_w, hidden_w, out_w, out_b)

    def _L1_cond_ref(x, cond, norm_w, up_w, down_w):
        import jax, jax.numpy as jnp
        import numpy as np
        EPS = 1e-06

        def act_quant(x):
            scale = 127.0 / jnp.clip(jnp.max(jnp.abs(x), axis=-1, keepdims=True), 1e-05, None)
            return jnp.clip(jnp.round(x * scale), -128.0, 127.0) / scale

        def weight_quant(w):
            scale = 1.0 / jnp.clip(jnp.mean(jnp.abs(w)), 1e-05, None)
            return jnp.clip(jnp.round(w * scale), -1.0, 1.0) / scale
        scale = cond @ norm_w.T + 1.0
        ms = jnp.mean(x * x, axis=-1, keepdims=True)
        h = x * (scale[:, None, :] * jax.lax.rsqrt(ms + EPS))
        u = h @ up_w.T
        val, gate = jnp.split(u, 2, axis=-1)
        h = val * jax.nn.gelu(gate, approximate=False)
        hq = h + jax.lax.stop_gradient(act_quant(h) - h)
        wq = down_w + jax.lax.stop_gradient(weight_quant(down_w) - down_w)
        y = hq @ wq.T
        return y + x
    x = _L0_cond_ref(x, cond_256, L0_cond_attn_gamma_w, L0_cond_attn_beta_w, L0_cond_W_q, L0_cond_W_k, L0_cond_W_v, L0_cond_W_o, L0_cond_attn_alpha_w, L0_cond_ffn_gamma_w, L0_cond_ffn_beta_w, L0_cond_gate_w, L0_cond_hidden_w, L0_cond_out_w, L0_cond_out_b, L0_cond_ffn_alpha_w)
    x = _L1_cond_ref(x, cond_256, L1_cond_norm_w, L1_cond_up_w, L1_cond_down_w)
    return x

_drawn_inputs = setup_inputs


def setup_inputs(seed=0):
    import zlib

    import numpy as np

    out = dict(_drawn_inputs(seed))
    spreads = {'L0_cond_out_b': (0.0, 0.1)}
    factors = {}
    for name, (base, spread) in spreads.items():
        noise = np.random.default_rng([zlib.crc32(name.encode()), seed]).standard_normal(out[name].shape)
        drawn = base * np.exp(spread * noise) if base else spread * noise
        out[name] = jnp.asarray(drawn.astype(out[name].dtype))
    for name, factor in factors.items():
        out[name] = (out[name] * factor).astype(out[name].dtype)
    return out
```

```python
from contextlib import ExitStack

import concourse.bass as bass
from concourse import mybir

F32 = mybir.dt.float32
F32R = mybir.dt.float32r
F16 = mybir.dt.float16
BF16 = mybir.dt.bfloat16
ALU = mybir.AluOpType
ACT = mybir.ActivationFunctionType
AX_X = mybir.AxisListType.X

P = 128
EPS = 1e-6
QUANT_EPS = 1e-5
ROUND = 12582912.0
P_SHIFT = 6.931471805599453


def build(nc, x, cond, w, out):
    B, S, D = x.shape
    C = cond.shape[1]
    F = w["gate_w"].shape[0]
    H = 16
    DH = D // H
    SCALE = (H / D) ** 0.5
    KD = D // P
    KF = F // P
    TT = S // P
    HT = P // DH
    NPART = 3
    KROWS = 6 * DH
    VW = NPART * DH + 1
    Q_PARTS = (0, 1, 2, 0, 1, 0)
    K_PARTS = (0, 0, 0, 1, 1, 2)
    NCH = 2 * KF
    HALF = S // 2

    KINDS = ("attn_gamma_w", "attn_beta_w", "ffn_gamma_w", "ffn_beta_w", "norm_w", "attn_alpha_w", "ffn_alpha_w")
    NSC = 5

    with ExitStack() as ctx:
        def sb(name, shape, dt=F32):
            return ctx.enter_context(nc.sbuf_tensor(name, shape, dt))

        def ps(name, shape, dt=F32):
            return ctx.enter_context(nc.psum_tensor(name, shape, dt))

        def sem(name):
            return ctx.enter_context(nc.semaphore(name))

        parts_d = nc.dram_tensor("parts_d", (2, NPART, D, S), BF16).ap()
        shift_d = nc.dram_tensor("shift_d", (NPART, H * TT, P), BF16).ap()
        alpha_d = nc.dram_tensor("alpha_d", (B, 3 * D), F32).ap()
        x2_d = nc.dram_tensor("x2_d", (B, S, D), F32).ap()

        wqkv = [sb(f"wqkv{i}", [P, KD, 3 * D], F32R) for i in range(2)]
        wo = [sb(f"wo{i}", [P, KD, D], F32R) for i in range(2)]
        wgh = [sb(f"wgh{i}", [P, KD, 2 * F], F32R) for i in range(2)]
        wout = [sb(f"wout{i}", [P, KF, D], F32R) for i in range(2)]
        wup = wgh
        wdown = sb("wdown", [P, KF, D], BF16)
        ident = sb("ident", [P, P], F32)
        ident_bf = sb("ident_bf", [P, P], BF16)
        ones = sb("ones", [P, P], F32)
        half_pow = sb("half_pow", [P, TT], F32)
        condr = sb("condr", [B, C])
        condT = sb("condT", [C, B])
        cw = sb("cw", [P, len(KINDS), KD, C])
        cwT = sb("cwT", [C, len(KINDS), D])
        table = sb("table", [P, NSC * KD, B])
        arow = sb("arow", [B, 3 * D])
        obrow = sb("obrow", [B, D])
        cur = sb("cur", [P, NSC * KD])
        wabs = sb("wabs", [P, 1])
        wmean = sb("wmean", [P, 1])
        winv = sb("winv", [P, 1])
        wdeq = sb("wdeq", [P, 1])

        xa = sb("xa", [P, TT, D])
        xr = sb("xr", [P, TT, D])
        x1 = sb("x1", [P, TT, D])
        al = sb("al", [P, 3 * D])
        xn = sb("xn", [P, TT, D])
        stat = sb("stat", [P, 3, TT])
        h32 = sb("h32", [P, KD, S])
        hs = [sb(f"hs{i}", [P, KD, S], F32R) for i in range(2)]
        qk3 = sb("qk3", [P, 2 * KD, NPART, S], BF16)
        qkres = sb("qkres", [P, 2, S])
        qst = sb("qst", [P, H, S], BF16)
        kst = sb("kst", [P, H, S], BF16)
        vst = sb("vst", [P, TT, H, VW], BF16)
        negmax = sb("negmax", [P, H, TT])
        shift32 = sb("shift32", [H * TT, 3, P])
        shift3 = sb("shift3", [H * TT, NPART, P], BF16)
        NP_BUF = 2
        p32 = sb("p32", [P, 2, 2 * S])
        ph = sb("ph", [P, NP_BUF, 2 * S], F16)
        pl = sb("pl", [P, NP_BUF, 2 * S], F16)
        osum = sb("osum", [P, 2, TT, DH])
        orec = sb("orec", [P, 2, TT])
        o = sb("o", [P, TT, D])
        oT = hs
        th = sb("th", [P, 2, HALF])
        ug = sb("ug", [P, 2, HALF])
        a32 = sb("a32", [P, 2, HALF])
        a2 = [sb(f"a2{i}", [P, 2, HALF], F32R) for i in range(2)]
        ge = p32
        hb = [qst[:, 4 * i:4 * i + 4, :].bitcast(F32).rearrange("p a b -> p (a b)") for i in range(2)]
        q32 = [qst[:, 8 + 4 * i:12 + 4 * i, :].bitcast(F32).rearrange("p a b -> p (a b)") for i in range(2)]
        qi = [kst[:, 2 * i:2 * i + 2, :].rearrange("p a b -> p (a b)") for i in range(2)]
        qT = [kst[:, 4 + 2 * i:6 + 2 * i, :].rearrange("p a b -> p (a b)") for i in range(2)]
        qs = sb("qs", [P, 2, 4])

        stage_q = qst[:, :, :].rearrange("p h t -> p (h t)").bitcast(F32)
        stage_k = kst[:, :, :].rearrange("p h t -> p (h t)").bitcast(F32)
        raw_qkvo = stage_q[:, 0:4 * KD * D].rearrange("p (n i) -> p n i", i=D)
        raw_out = stage_q[:, 4 * KD * D:4 * KD * D + KD * F].rearrange("p (n i) -> p n i", i=F)
        raw_gh = stage_k.rearrange("p (n i) -> p n i", i=D)
        raw_up = stage_q.rearrange("p (n i) -> p n i", i=D)
        raw_down = stage_k[:, 0:KD * F]
        tern_t = stage_k[:, KD * F:2 * KD * F]
        tern = tern_t.bitcast(BF16)[:, 0:KD * F]

        big = ps("big", [P, 2, 2 * S])
        pvb = [ps(f"pvb{i}", [P, 512]) for i in range(2)]
        gen = [ps(f"gen{i}", [P, 512]) for i in range(2)]
        big_flat = big[:, :, :].rearrange("p a b -> p (a b)")
        wbank = gen + pvb

        names = """past raw_load raw_up_load raw_down_load cond_load ob_load ident_set consts_set cond_t cond_tc cw_t cw_tc
        tab_mm tab_copy row_mm row_copy row_ob alpha_stored kones
        wt_t wt_hi wt_lo cur_set
        xa_load xr_load al_load sq1 ms1 rs1 xn1 xt1 h32_1 hh1 hl1
        qk_mm qk_h qk_r qk_m qk_l v_mm v_h v_r v_m v_l parts_st stack_ld
        smax_mm smax shift_t shift_c shift_st shift_ld
        st_mm exp_ ph_ pl_pool pl_dve pv_mm o_sum o_rec o_norm
        o_t oh ol oproj xt_ x1_ x1b sq2 ms2 rs2 xn2 xt2 h32_2 hh2 hl2
        gh_mm tanh_ u_ a_ ah a_lo y_mm yt x2_ x2_st
        wsum wsum_mm wq_ tern tern_t_ tern_c up_t up_hi up_lo
        x2_ld sq3 ms3 rs3 xn3 xt3 h32_3 hh3 hl3 g_mm v2_mm gelu hmul amax qscale q32_ qi_ q_t q_tc d_mm final out_st
        """.split()
        s = {n: sem(n) for n in names}

        def need(eng, name, per, b, k):
            v = b * per + k
            if isinstance(v, int) and v <= 0:
                return
            eng.wait_ge(s[name], v)

        def past(eng, b):
            if not isinstance(b, int):
                eng.sem_inc(s["past"], 1)

        def groups(raw, rows, kchunks, dst):
            tiles = [(r, k) for k in range(kchunks) for r in range(rows)]
            return [([raw(r, k) for r, k in tiles[4 * g:4 * g + 4]],
                     [t[:, :, :].rearrange("p k n -> p (k n)")[:, 512 * g:512 * g + 512] for t in dst])
                    for g in range(len(tiles) // 4)]

        def cols(raw):
            return lambda r, k: raw[:, r, k * P:(k + 1) * P]

        WG = (groups(cols(raw_qkvo), 3 * KD, KD, wqkv)
              + groups(cols(raw_qkvo[:, 3 * KD:4 * KD, :]), KD, KD, wo)
              + groups(cols(raw_gh), 2 * KF, KD, wgh)
              + groups(cols(raw_out), KD, KF, wout))
        WG_UP = groups(cols(raw_up), 2 * KF, KD, wup)

        block = ctx.enter_context(nc.Block())

        def rows_of(t, b):
            return t[bass.ds(b, 1), :, :].rearrange("o (t p) d -> p (o t) d", p=P)

        @block.sync
        def _(sp):
            def need_sp(name, per, b, k):
                need(sp, name, per, b, k)
                past(sp, b)

            sp.dma_start(condr[:, :], cond).then_inc(s["cond_load"], 16)
            for i, n in enumerate(KINDS):
                sp.dma_start(cw[:, i, :, :], w[n].rearrange("(k p) c -> p k c", p=P)).then_inc(s["cond_load"], 16)
            sp.dma_start(obrow[:, :], w["out_b"].rearrange("(o d) -> o d", o=1).broadcast_to([B, D])).then_inc(s["ob_load"], 16)
            for i, n in enumerate(("W_q", "W_k", "W_v", "W_o")):
                sp.dma_start(raw_qkvo[:, KD * i:KD * i + KD, :], w[n].rearrange("(r p) i -> p r i", p=P)).then_inc(s["raw_load"], 16)
            for i, n in enumerate(("gate_w", "hidden_w")):
                sp.dma_start(raw_gh[:, KF * i:KF * i + KF, :], w[n].rearrange("(r p) i -> p r i", p=P)).then_inc(s["raw_load"], 16)
            sp.dma_start(raw_out, w["out_w"].rearrange("(r p) i -> p r i", p=P)).then_inc(s["raw_load"], 16)
            sp.wait_ge(s["row_ob"], 1)
            sp.dma_start(alpha_d, arow[:, :]).then_inc(s["alpha_stored"], 16)
            sp.wait_ge(s["alpha_stored"], 16)

            def sequence(b):
                need_sp("sq1", TT, b, 0)
                need_sp("xn1", TT, b, 0)
                sp.dma_start(xa[:, :, :], rows_of(x, b)).then_inc(s["xa_load"], 16)
                need_sp("x1_", 2, b, 0)
                sp.dma_start(xr[:, :, :], rows_of(x, b)).then_inc(s["xr_load"], 16)
                need_sp("yt", 2, b, 0)
                need_sp("x1b", 1, b, 0)
                sp.dma_start(al[:, :], alpha_d[bass.ds(b, 1), :].broadcast_to([P, 3 * D])).then_inc(s["al_load"], 16)
                need_sp("stack_ld", 192, b, 0)
                for j in range(2 * KD):
                    need_sp("qk_l", 4, b, j + 1)
                    sp.dma_start(parts_d[j // KD, :, (j % KD) * P:(j % KD + 1) * P, :].rearrange("n p t -> p n t"),
                                 qk3[:, j, :, :]).then_inc(s["parts_st"], 16)
                need_sp("parts_st", 16 * 2 * KD, b, 16 * 2 * KD)
                need_sp("st_mm", 2 * H, b, 0)
                if isinstance(b, int) and b == 0:
                    sp.wait_ge(s["wt_hi"], len(WG))
                for st, which, parts in ((qst, 0, Q_PARTS), (kst, 1, K_PARTS)):
                    for g, part in enumerate(parts):
                        sp.dma_start(st[g * DH:(g + 1) * DH, :, :],
                                     parts_d[which, part].rearrange("(h d) t -> d h t", d=DH)).then_inc(s["stack_ld"], 16)
                need_sp("shift_c", 5, b, 5)
                sp.dma_start(shift_d.rearrange("n m t -> m n t"), shift3[:, :, :]).then_inc(s["shift_st"], 16)
                need_sp("shift_st", 16, b, 16)
                sp.dma_start(qst[KROWS:KROWS + NPART, :, :], shift_d.rearrange("n (h j) t -> n h (j t)", h=H)).then_inc(s["shift_ld"], 16)
                need_sp("x2_", 2, b, 2)
                sp.dma_start(rows_of(x2_d, b), x1[:, :, :]).then_inc(s["x2_st"], 16)

            sequence(0)
            with sp.Fori(1, B) as b:
                sequence(b)

            sp.wait_ge(s["st_mm"], 2 * H * B)
            sp.dma_start(raw_down.rearrange("p (r i) -> p r i", i=F), w["down_w"].rearrange("(r p) i -> p r i", p=P)).then_inc(s["raw_down_load"], 16)
            sp.dma_start(raw_up, w["up_w"].rearrange("(r p) i -> p r i", p=P)).then_inc(s["raw_up_load"], 16)
            sp.wait_ge(s["x2_st"], 16 * B)

            def sequence_b(b):
                need_sp("sq3", TT, b, 0)
                need_sp("xn3", TT, b, 0)
                sp.dma_start(xa[:, :, :], rows_of(x2_d, b)).then_inc(s["x2_ld"], 16)
                need_sp("final", TT, b, 0)
                sp.dma_start(xr[:, :, :], rows_of(x2_d, b)).then_inc(s["xr_load"], 16)
                need_sp("final", TT, b, TT)
                sp.dma_start(rows_of(out, b), x1[:, :, :]).then_inc(s["out_st"], 16)

            sequence_b(0)
            with sp.Fori(1, B) as b:
                sequence_b(b)
            sp.wait_ge(s["out_st"], 16 * B)

        @block.gpsimd
        def _(pool):
            pool.memset(ident[:, :], 0.0).then_inc(s["ident_set"], 1)
            pool.memset(ident_bf[:, :], 0.0).then_inc(s["ident_set"], 1)
            pool.wait_ge(s["ident_set"], 2)
            for m in (ident, ident_bf):
                pool.affine_select(out=m[:, :], in_=m[:, :], compare_op=ALU.not_equal, fill=1.0, base=0,
                                   pattern=[[-1, P]], channel_multiplier=1).then_inc(s["ident_set"], 1)
            pool.memset(ones[:, :], 1.0).then_inc(s["consts_set"], 1)
            pool.memset(half_pow[:, :], -0.5).then_inc(s["consts_set"], 1)
            pool.memset(vst[:, :, :, VW - 1:VW], 1.0).then_inc(s["consts_set"], 1)
            pool.wait_ge(s["consts_set"], 3)
            pool.wait_ge(s["wt_lo"], len(WG))
            pool.memset(kst[KROWS:KROWS + NPART, :, :], 1.0).then_inc(s["kones"], 1)
            pool.wait_ge(s["kones"], 1)

            def rstd(b, i):
                need(pool, f"sq{i}", TT, b, TT)
                past(pool, b)
                pool.tensor_scalar(stat[:, 1, :], stat[:, 0, :], 1.0 / D, EPS, ALU.mult, ALU.add).then_inc(s[f"ms{i}"], 1)
                need(pool, f"ms{i}", 1, b, 1)
                pool.tensor_tensor(stat[:, 2, :], stat[:, 1, :], half_pow[:, :], ALU.pow).then_inc(s[f"rs{i}"], 1)

            def h_lo(b, i):
                for k in range(KD):
                    need(pool, f"hh{i}", KD, b, k + 1)
                    pool.tensor_tensor(hs[1][:, k, :], h32[:, k, :], hs[0][:, k, :].bitcast(F32), ALU.subtract).then_inc(s[f"hl{i}"], 1)

            def sequence(b):
                rstd(b, 1)
                h_lo(b, 1)
                for j in range(2 * KD):
                    need(pool, "qk_r", 2 * KD, b, j + 1)
                    past(pool, b)
                    pool.tensor_scalar(qk3[:, j, 1, :], qkres[:, j % 2, :], 1.0, 0.0, ALU.mult, ALU.add).then_inc(s["qk_m"], 1)
                    need(pool, "qk_m", 2 * KD, b, j + 1)
                    pool.tensor_tensor(qk3[:, j, 2, :], qkres[:, j % 2, :], qk3[:, j, 1, :], ALU.subtract).then_inc(s["qk_l"], 1)
                for t in range(TT):
                    need(pool, "v_r", TT // 2, b, t // 2 + 1)
                    past(pool, b)
                    res = qkres[:, t // 2, :].rearrange("p (t h d) -> p t h d", t=2, h=H)[:, t % 2]
                    pool.tensor_scalar(vst[:, t, :, DH:2 * DH], res, 1.0, 0.0, ALU.mult, ALU.add).then_inc(s["v_m"], 1)
                    need(pool, "v_m", TT, b, t + 1)
                    pool.tensor_tensor(vst[:, t, :, 2 * DH:3 * DH], res, vst[:, t, :, DH:2 * DH], ALU.subtract).then_inc(s["v_l"], 1)
                for m in range(0, 2 * H, 2):
                    need(pool, "ph_", 2 * H, b, m + 1)
                    need(pool, "pv_mm", 2 * H, b, m - 1)
                    pool.tensor_tensor(pl[:, m % 2, :], p32[:, m % 2, :], ph[:, m % 2, :], ALU.subtract).then_inc(s["pl_pool"], 1)
                rstd(b, 2)
                need(pool, "xn2", TT, b, TT)
                need(pool, "al_load", 16, b, 16)
                pool.tensor_tensor(x1[:, :, :], x1[:, :, :], al[:, 2 * D:3 * D].unsqueeze(1).broadcast_to([P, TT, D]), ALU.add).then_inc(s["x1b"], 1)
                h_lo(b, 2)
                for n in range(NCH):
                    need(pool, "ah", NCH, b, n + 1)
                    need(pool, "y_mm", NCH, b, n - 1)
                    pool.tensor_tensor(a2[1][:, n % 2, :], a32[:, n % 2, :], a2[0][:, n % 2, :].bitcast(F32), ALU.subtract).then_inc(s["a_lo"], 1)

            sequence(0)
            with pool.Fori(1, B) as b:
                sequence(b)

            def sequence_b(b):
                rstd(b, 3)
                need(pool, "v2_mm", 2 * TT, b, 0)
                h_lo(b, 3)
                for t in range(TT):
                    need(pool, "q32_", TT, b, t + 1)
                    need(pool, "q_t", TT, b, t - 1)
                    past(pool, b)
                    pool.tensor_scalar(qi[t % 2], q32[t % 2], -ROUND, 1.0, ALU.add, ALU.mult).then_inc(s["qi_"], 1)

            sequence_b(0)
            with pool.Fori(1, B) as b:
                sequence_b(b)

        @block.scalar
        def _(act):
            def split_hi(gs, t_sem, hi_sem, lo_sem):
                for g, (_, dst) in enumerate(gs):
                    act.wait_ge(s[t_sem], g + 1)
                    act.copy(dst[0], wbank[g % 4][:, :]).then_inc(s[hi_sem], 1)

            split_hi(WG, "wt_t", "wt_hi", "wt_lo")

            def squares(b, i, src):
                for t in range(TT):
                    act.activation(xn[:, t, :], src[:, t, :], ACT.Square, accum_out=stat[:, 0, t:t + 1]).then_inc(s[f"sq{i}"], 1)

            def h_hi(b, i):
                for k in range(KD):
                    need(act, f"h32_{i}", KD, b, k + 1)
                    act.copy(hs[0][:, k, :], h32[:, k, :]).then_inc(s[f"hh{i}"], 1)

            def sequence(b):
                need(act, "xa_load", 16, b, 16)
                squares(b, 1, xa)
                h_hi(b, 1)
                need(act, "parts_st", 16 * 2 * KD, b, 0)
                for j in range(2 * KD):
                    need(act, "qk_mm", 2 * KD, b, j + 1)
                    act.copy(qk3[:, j, 0, :], gen[j % 2][:, :]).then_inc(s["qk_h"], 1)
                for j in range(TT // 2):
                    need(act, "v_mm", TT // 2, b, j + 1)
                    act.copy(vst[:, 2 * j:2 * j + 2, :, 0:DH], gen[j][:, :].rearrange("p (t h d) -> p t h d", t=2, h=H)).then_inc(s["v_h"], 1)

                def exp(m):
                    need(act, "st_mm", 2 * H, b, m + 1)
                    need(act, ("pl_pool", "pl_dve")[m % 2], H, b, m // 2)
                    need(act, "ph_", 2 * H, b, m - 1)
                    act.activation(p32[:, m % 2, :], big[:, m % 2, :], ACT.Exp, scale=SCALE).then_inc(s["exp_"], 1)

                exp(0)
                for m in range(2 * H):
                    if m + 1 < 2 * H:
                        exp(m + 1)
                    need(act, "exp_", 2 * H, b, m + 1)
                    need(act, "pv_mm", 2 * H, b, m - 1)
                    act.copy(ph[:, m % 2, :], p32[:, m % 2, :]).then_inc(s["ph_"], 1)
                for k in range(KD):
                    need(act, "o_t", KD, b, k + 1)
                    act.copy(hs[0][:, k, :], gen[k][:, :]).then_inc(s["oh"], 1)
                need(act, "x1_", 2, b, 2)
                squares(b, 2, x1)
                h_hi(b, 2)

                def tanh(n):
                    need(act, "gh_mm", NCH, b, n + 1)
                    need(act, "u_", NCH, b, n - 1)
                    act.activation(th[:, n % 2, :], big[:, n % 2, 0:HALF], ACT.Tanh, scale=0.5).then_inc(s["tanh_"], 1)

                tanh(0)
                for n in range(NCH):
                    if n + 1 < NCH:
                        tanh(n + 1)
                    need(act, "a_", NCH, b, n + 1)
                    need(act, "y_mm", NCH, b, n - 1)
                    act.copy(a2[0][:, n % 2, :], a32[:, n % 2, :]).then_inc(s["ah"], 1)

            sequence(0)
            with act.Fori(1, B) as b:
                sequence(b)

            split_hi(WG_UP, "up_t", "up_hi", "up_lo")

            def sequence_b(b):
                need(act, "x2_ld", 16, b, 16)
                squares(b, 3, xa)
                need(act, "v2_mm", 2 * TT, b, 0)
                h_hi(b, 3)
                for i in range(2 * TT):
                    need(act, "g_mm", 2 * TT, b, i + 1)
                    need(act, "hmul", 2 * TT, b, i - 1)
                    act.activation(ge[:, i % 2, 0:S], big[:, 0, i % 2 * S:i % 2 * S + S], ACT.Gelu).then_inc(s["gelu"], 1)

            sequence_b(0)
            with act.Fori(1, B) as b:
                sequence_b(b)

        @block.vector
        def _(dve):
            dve.wait_ge(s["cond_t"], 1)
            dve.tensor_copy(condT[:, :], gen[0][0:C, 0:B]).then_inc(s["cond_tc"], 1)
            dve.wait_ge(s["cw_t"], 1)
            n_cw = len(KINDS) * D
            dve.tensor_copy(cwT[:, :, :].rearrange("c n d -> c (n d)"), big_flat[0:C, 0:n_cw]).then_inc(s["cw_tc"], 1)
            dve.wait_ge(s["tab_mm"], 1)
            nt = NSC * KD
            dve.tensor_copy(table[:, 0:nt - KD, :].rearrange("p n b -> p (n b)"), gen[1][:, 0:(nt - KD) * B]).then_inc(s["tab_copy"], 1)
            dve.tensor_scalar(table[:, nt - KD:nt, :].rearrange("p n b -> p (n b)"), gen[1][:, (nt - KD) * B:nt * B], 1.0, None, ALU.add).then_inc(s["tab_copy"], 1)
            dve.wait_ge(s["row_mm"], 1)
            dve.tensor_copy(arow[:, 0:2 * D], pvb[0][0:B, :]).then_inc(s["row_copy"], 1)
            dve.wait_ge(s["row_copy"], 1)
            dve.wait_ge(s["ob_load"], 16)
            dve.tensor_tensor(arow[:, 2 * D:3 * D], arow[:, D:2 * D], obrow[:, :], ALU.mult).then_inc(s["row_ob"], 1)

            def split_lo(gs, hi_sem, lo_sem):
                for g, (_, dst) in enumerate(gs):
                    dve.wait_ge(s[hi_sem], g + 1)
                    dve.tensor_tensor(dst[1], wbank[g % 4][:, :], dst[0].bitcast(F32), ALU.subtract).then_inc(s[lo_sem], 1)

            split_lo(WG, "wt_hi", "wt_lo")
            dve.wait_ge(s["tab_copy"], 2)

            def xnorm(b, i, src):
                need(dve, f"rs{i}", 1, b, 1)
                for t in range(TT):
                    dve.tensor_scalar(xn[:, t, :], src[:, t, :], stat[:, 2, t:t + 1], None, ALU.mult).then_inc(s[f"xn{i}"], 1)

            def affine(b, i, gamma, beta):
                for k in range(KD):
                    need(dve, f"xt{i}", KD, b, k + 1)
                    scale = cur[:, gamma * KD + k:gamma * KD + k + 1]
                    if beta is None:
                        dve.tensor_scalar(h32[:, k, :], gen[k][:, :], scale, None, ALU.mult).then_inc(s[f"h32_{i}"], 1)
                    else:
                        dve.tensor_scalar(h32[:, k, :], gen[k][:, :], scale, cur[:, beta * KD + k:beta * KD + k + 1],
                                          ALU.mult, ALU.add).then_inc(s[f"h32_{i}"], 1)

            def two(t, i):
                return t[:, i, :].rearrange("p (t d) -> p t d", t=2)

            def scaled(b, i, name, src, col):
                dve.tensor_tensor(two(h32, i), src[i][:, :].rearrange("p (t d) -> p t d", t=2),
                                  al[:, col:col + D].unsqueeze(1).broadcast_to([P, 2, D]), ALU.mult).then_inc(s[name], 1)

            def sequence(b):
                dve.tensor_copy(cur[:, :].unsqueeze(2), table[:, :, bass.ds(b, 1)]).then_inc(s["cur_set"], 1)
                xnorm(b, 1, xa)
                need(dve, "cur_set", 1, b, 1)
                affine(b, 1, 0, 1)
                for j in range(2 * KD):
                    need(dve, "qk_h", 2 * KD, b, j + 1)
                    need(dve, "qk_l", 2 * KD, b, j - 1)
                    dve.tensor_tensor(qkres[:, j % 2, :], gen[j % 2][:, :], qk3[:, j, 0, :], ALU.subtract).then_inc(s["qk_r"], 1)
                for j in range(TT // 2):
                    need(dve, "v_h", TT // 2, b, j + 1)
                    need(dve, "qk_l", 2 * KD, b, 2 * KD - 1 + j)
                    dve.tensor_tensor(qkres[:, j, :].rearrange("p (t h d) -> p t h d", t=2, h=H),
                                      gen[j][:, :].rearrange("p (t h d) -> p t h d", t=2, h=H),
                                      vst[:, 2 * j:2 * j + 2, :, 0:DH], ALU.subtract).then_inc(s["v_r"], 1)
                for n in range(2 * H):
                    need(dve, "smax_mm", 2 * H, b, n + 1)
                    h, i = n // 2, n % 2
                    dve.tensor_reduce(negmax[:, h, 2 * i:2 * i + 2], big[:, n % 2, :].rearrange("p (a k) -> p a k", a=2),
                                      AX_X, ALU.max, negate=True).then_inc(s["smax"], 1)
                need(dve, "shift_t", 1, b, 1)
                M = H * TT
                dve.tensor_scalar(shift32[:, 0, :], gen[0][0:M, 0:P], P_SHIFT / SCALE, None, ALU.add).then_inc(s["shift_c"], 1)
                need(dve, "shift_c", 5, b, 1)
                dve.tensor_copy(shift3[:, 0, :], shift32[:, 0, :]).then_inc(s["shift_c"], 1)
                need(dve, "shift_c", 5, b, 2)
                dve.tensor_tensor(shift32[:, 1, :], shift32[:, 0, :], shift3[:, 0, :], ALU.subtract).then_inc(s["shift_c"], 1)
                need(dve, "shift_c", 5, b, 3)
                dve.tensor_copy(shift3[:, 1, :], shift32[:, 1, :]).then_inc(s["shift_c"], 1)
                need(dve, "shift_c", 5, b, 4)
                dve.tensor_tensor(shift3[:, 2, :], shift32[:, 1, :], shift3[:, 1, :], ALU.subtract).then_inc(s["shift_c"], 1)

                def p_lo(m):
                    need(dve, "ph_", 2 * H, b, m + 1)
                    need(dve, "pv_mm", 2 * H, b, m - 1)
                    dve.tensor_tensor(pl[:, m % 2, :], p32[:, m % 2, :], ph[:, m % 2, :], ALU.subtract).then_inc(s["pl_dve"], 1)

                def head_out(h):
                    need(dve, "pv_mm", 2 * H, b, 2 * h + 2)
                    pv = pvb[h % 2][:, 0:TT * VW].rearrange("p (q w) -> p q w", w=VW)
                    dve.tensor_reduce(osum[:, h % 2], pv[:, :, 0:NPART * DH].rearrange("p q (n d) -> p q d n", n=NPART),
                                      AX_X, ALU.add).then_inc(s["o_sum"], 1)
                    dve.reciprocal(orec[:, h % 2, :].unsqueeze(2), pv[:, :, VW - 1:VW]).then_inc(s["o_rec"], 1)
                    need(dve, "o_sum", H, b, h + 1)
                    need(dve, "o_rec", H, b, h + 1)
                    dve.tensor_tensor(o[:, :, h * DH:(h + 1) * DH], osum[:, h % 2],
                                      orec[:, h % 2, :].unsqueeze(2).broadcast_to([P, TT, DH]), ALU.mult).then_inc(s["o_norm"], 1)

                for h in range(H):
                    p_lo(2 * h + 1)
                    if h >= 1:
                        head_out(h - 1)
                head_out(H - 1)
                for k in range(KD):
                    need(dve, "oh", KD, b, k + 1)
                    dve.tensor_tensor(hs[1][:, k, :], gen[k][:, :], hs[0][:, k, :].bitcast(F32), ALU.subtract).then_inc(s["ol"], 1)
                need(dve, "al_load", 16, b, 16)
                need(dve, "xr_load", 16, b, 16)
                need(dve, "x2_st", 16, b, 0)
                for i in range(2):
                    need(dve, "oproj", 2, b, i + 1)
                    scaled(b, i, "xt_", gen, 0)
                    need(dve, "xt_", 2, b, i + 1)
                    dve.tensor_tensor(x1[:, 2 * i:2 * i + 2, :], two(h32, i), xr[:, 2 * i:2 * i + 2, :], ALU.add).then_inc(s["x1_"], 1)
                xnorm(b, 2, x1)
                affine(b, 2, 2, 3)
                for n in range(NCH):
                    need(dve, "tanh_", NCH, b, n + 1)
                    dve.scalar_tensor_tensor(out=ug[:, n % 2, :], in0=th[:, n % 2, :], scalar=1.0,
                                             in1=big[:, n % 2, 0:HALF], op0=ALU.add, op1=ALU.mult).then_inc(s["u_"], 1)
                    need(dve, "u_", NCH, b, n + 1)
                    need(dve, "a_lo", NCH, b, n - 1)
                    dve.scalar_tensor_tensor(out=a32[:, n % 2, :], in0=ug[:, n % 2, :], scalar=0.5,
                                             in1=big[:, n % 2, HALF:2 * HALF], op0=ALU.mult, op1=ALU.mult).then_inc(s["a_"], 1)
                need(dve, "x1b", 1, b, 1)
                for i in range(2):
                    need(dve, "y_mm", NCH, b, KF * (i + 1))
                    scaled(b, i, "yt", gen, D)
                    need(dve, "yt", 2, b, i + 1)
                    dve.tensor_tensor(x1[:, 2 * i:2 * i + 2, :], two(h32, i), x1[:, 2 * i:2 * i + 2, :], ALU.add).then_inc(s["x2_"], 1)

            sequence(0)
            with dve.Fori(1, B) as b:
                sequence(b)

            dve.wait_ge(s["raw_down_load"], 16)
            dve.tensor_reduce(wabs[:, :], raw_down, AX_X, ALU.add, apply_absolute_value=True).then_inc(s["wsum"], 1)
            dve.wait_ge(s["wsum_mm"], 1)
            dve.tensor_scalar(wmean[:, :], gen[0][:, 0:1], 1.0 / (D * F), QUANT_EPS, ALU.mult, ALU.max).then_inc(s["wq_"], 1)
            dve.wait_ge(s["wq_"], 1)
            dve.reciprocal(winv[:, :], wmean[:, :]).then_inc(s["wq_"], 1)
            dve.wait_ge(s["wq_"], 2)
            dve.tensor_scalar(tern_t, raw_down, winv[:, 0:1], 1.0, ALU.mult, ALU.min).then_inc(s["wq_"], 1)
            dve.wait_ge(s["wq_"], 3)
            dve.tensor_scalar(raw_down, tern_t, -1.0, ROUND, ALU.max, ALU.add).then_inc(s["wq_"], 1)
            dve.wait_ge(s["wq_"], 4)
            dve.tensor_scalar(tern, raw_down, ROUND, None, ALU.subtract).then_inc(s["tern"], 1)
            dve.wait_ge(s["tern_t_"], 1)
            dve.tensor_copy(wdown[:, :, :].rearrange("p k n -> p (k n)"), big[:, 0, :].bitcast(BF16)).then_inc(s["tern_c"], 1)
            split_lo(WG_UP, "up_hi", "up_lo")

            def sequence_b(b):
                dve.tensor_copy(cur[:, :].unsqueeze(2), table[:, :, bass.ds(b, 1)]).then_inc(s["cur_set"], 1)
                xnorm(b, 3, xa)
                need(dve, "cur_set", 1, b + B, 1)
                affine(b, 3, 4, None)

                def h_mul(i):
                    t, c = i // 2, i % 2
                    need(dve, "gelu", 2 * TT, b, i + 1)
                    need(dve, "v2_mm", 2 * TT, b, i + 1)
                    dve.tensor_tensor(hb[t % 2][:, c * S:(c + 1) * S], big[:, 1, i % 2 * S:i % 2 * S + S], ge[:, i % 2, 0:S], ALU.mult).then_inc(s["hmul"], 1)

                def quantise(t):
                    need(dve, "hmul", 2 * TT, b, 2 * t + 2)
                    q = [qs[:, t % 2, n:n + 1] for n in range(4)]
                    dve.tensor_reduce(q[0], hb[t % 2], AX_X, ALU.max, apply_absolute_value=True).then_inc(s["amax"], 1)
                    need(dve, "amax", TT, b, t + 1)
                    dve.tensor_scalar(q[1], q[0], QUANT_EPS, 1.0 / 127.0, ALU.max, ALU.mult).then_inc(s["qscale"], 1)
                    need(dve, "qscale", 3 * TT, b, 3 * t + 1)
                    dve.reciprocal(q[2], q[1]).then_inc(s["qscale"], 1)
                    dve.tensor_scalar(q[3], q[1], wmean[:, 0:1], None, ALU.mult).then_inc(s["qscale"], 1)
                    need(dve, "qscale", 3 * TT, b, 3 * t + 3)
                    need(dve, "qi_", TT, b, t - 1)
                    dve.tensor_scalar(q32[t % 2], hb[t % 2], q[2], ROUND, ALU.mult, ALU.add).then_inc(s["q32_"], 1)

                def q_copy(t):
                    need(dve, "q_t", TT, b, t + 1)
                    need(dve, "d_mm", TT, b, t - 1)
                    dve.tensor_scalar(qT[t % 2], pvb[t % 2][:, :].bitcast(BF16), 127.0, -128.0, ALU.min, ALU.max).then_inc(s["q_tc"], 1)

                def finish(t):
                    need(dve, "d_mm", TT, b, t + 1)
                    dve.scalar_tensor_tensor(out=x1[:, t, :], in0=gen[t % 2][:, 0:D], scalar=qs[:, t % 2, 3:4],
                                             in1=xr[:, t, :], op0=ALU.mult, op1=ALU.add).then_inc(s["final"], 1)

                h_mul(0)
                h_mul(1)
                quantise(0)
                need(dve, "xr_load", 16, b + B, 16)
                need(dve, "out_st", 16, b, 0)
                for t in range(1, TT):
                    h_mul(2 * t)
                    h_mul(2 * t + 1)
                    q_copy(t - 1)
                    if t >= 2:
                        finish(t - 2)
                    quantise(t)
                q_copy(TT - 1)
                finish(TT - 2)
                finish(TT - 1)

            dve.wait_ge(s["x2_st"], 16 * B)
            sequence_b(0)
            with dve.Fori(1, B) as b:
                sequence_b(b)

        @block.tensor
        def _(pe):
            def exact(out_, terms, start=True, stop=True, **kw):
                passes = [(l[a], r[c]) for l, r in terms for a, c in ((0, 0), (0, 1), (1, 0))]
                for i, (l, r) in enumerate(passes):
                    last = pe.matmul(out_, l, r, start=start and i == 0, stop=stop and i == len(passes) - 1, **kw)
                return last

            pe.wait_ge(s["ident_set"], 4)
            pe.wait_ge(s["cond_load"], 16 * (1 + len(KINDS)))
            pe.transpose(gen[0][0:C, 0:B], condr[:, :], ident[0:B, 0:B]).then_inc(s["cond_t"], 1)
            for i in range(len(KINDS)):
                for k in range(KD):
                    last = pe.transpose(big_flat[0:C, (i * KD + k) * P:(i * KD + k + 1) * P], cw[:, i, k, :], ident[:, :])
            last.then_inc(s["cw_t"], 1)
            pe.wait_ge(s["cond_tc"], 1)
            pe.wait_ge(s["cw_tc"], 1)
            for i in range(NSC):
                for k in range(KD):
                    n = i * KD + k
                    last = pe.matmul(gen[1][:, n * B:(n + 1) * B], cwT[:, i, k * P:(k + 1) * P], condT[:, :], start=True, stop=True)
            last.then_inc(s["tab_mm"], 1)
            pe.matmul(pvb[0][0:B, :], condT[:, :], cwT[:, NSC:NSC + 2, :].rearrange("c n d -> c (n d)"), start=True, stop=True).then_inc(s["row_mm"], 1)
            pe.wait_ge(s["tab_copy"], 2)
            pe.wait_ge(s["row_copy"], 1)

            def transpose_weights(gs, t_sem, lo_sem):
                for g, (src, _) in enumerate(gs):
                    if g >= 4:
                        pe.wait_ge(s[lo_sem], g - 3)
                    for i, a in enumerate(src):
                        last = pe.transpose(wbank[g % 4][:, i * P:(i + 1) * P], a, ident[:, :])
                    last.then_inc(s[t_sem], 1)

            pe.wait_ge(s["raw_load"], 16 * 7)
            transpose_weights(WG, "wt_t", "wt_lo")
            pe.wait_ge(s["wt_lo"], len(WG))
            pe.wait_ge(s["consts_set"], 3)

            def norm_t(b, i):
                need(pe, f"xn{i}", TT, b, TT)
                for k in range(KD):
                    for t in range(TT):
                        last = pe.transpose(gen[k][:, t * P:(t + 1) * P], xn[:, t, k * P:(k + 1) * P], ident[:, :])
                    last.then_inc(s[f"xt{i}"], 1)
                need(pe, f"hh{i}", KD, b, KD)
                need(pe, f"hl{i}", KD, b, KD)

            def col(pair, k, a, n):
                return [t[:, k, a:a + n] for t in pair]

            def sequence(b):
                norm_t(b, 1)
                for j in range(2 * KD):
                    if j >= 2:
                        need(pe, "qk_r", 2 * KD, b, j - 1)
                    exact(gen[j % 2][:, :], [(col(wqkv, k, j * P, P), col(hs, k, 0, S)) for k in range(KD)]).then_inc(s["qk_mm"], 1)
                for j in range(TT // 2):
                    need(pe, "qk_r", 2 * KD, b, 2 * KD - 1 + j)
                    for t in range(2):
                        last = exact(gen[j][:, t * D:(t + 1) * D],
                                     [(col(hs, k, (2 * j + t) * P, P), col(wqkv, k, 2 * D, D)) for k in range(KD)])
                    last.then_inc(s["v_mm"], 1)
                need(pe, "stack_ld", 192, b, 192)
                for n in range(2 * H):
                    h = n // 2
                    if n >= 2:
                        need(pe, "smax", 2 * H, b, n - 1)
                    for i in range(2):
                        q0 = (2 * (n % 2) + i) * P
                        last = pe.matmul(big[:, n % 2, i * S:(i + 1) * S], qst[0:KROWS, h, q0:q0 + P], kst[0:KROWS, h, :], start=True, stop=True)
                    last.then_inc(s["smax_mm"], 1)
                need(pe, "smax", 2 * H, b, 2 * H)
                need(pe, "v_r", TT // 2, b, TT // 2)
                past(pe, b)
                pe.transpose(gen[0][0:H * TT, 0:P], negmax[:, :, :].rearrange("p h t -> p (h t)"), ident[:, :]).then_inc(s["shift_t"], 1)
                need(pe, "shift_ld", 16, b, 16)
                if isinstance(b, int):
                    pe.wait_ge(s["kones"], 1)
                need(pe, "v_l", TT, b, TT)

                def scores(m):
                    h = m // 2
                    need(pe, "exp_", 2 * H, b, m - 1)
                    for i in range(2):
                        k0 = (2 * (m % 2) + i) * P
                        last = pe.matmul(big[:, m % 2, i * S:(i + 1) * S], kst[0:KROWS + NPART, h, k0:k0 + P],
                                         qst[0:KROWS + NPART, h, :], start=True, stop=True)
                    last.then_inc(s["st_mm"], 1)

                def weighted(m):
                    h = m // 2
                    if m % 2 == 0:
                        need(pe, "o_rec", H, b, h - 1)
                    need(pe, "ph_", 2 * H, b, m + 1)
                    need(pe, ("pl_pool", "pl_dve")[m % 2], H, b, m // 2 + 1)
                    for q in range(TT):
                        for i in range(2):
                            for part in (ph, pl):
                                a = i * S + q * P
                                last = pe.matmul(pvb[h % 2][:, q * VW:(q + 1) * VW], part[:, m % 2, a:a + P], vst[:, 2 * (m % 2) + i, h, :],
                                                 start=(m % 2 == 0 and q == 0 and i == 0 and part is ph),
                                                 stop=(m % 2 == 1 and i == 1 and part is pl), skip_group_check=True)
                    last.then_inc(s["pv_mm"], 1)

                scores(0)
                scores(1)
                for m in range(2 * H):
                    if m + 2 < 2 * H:
                        scores(m + 2)
                    weighted(m)
                need(pe, "o_norm", H, b, H)
                for k in range(KD):
                    for t in range(TT):
                        last = pe.transpose(gen[k][:, t * P:(t + 1) * P], o[:, t, k * P:(k + 1) * P], ident[:, :])
                    last.then_inc(s["o_t"], 1)
                need(pe, "oh", KD, b, KD)
                need(pe, "ol", KD, b, KD)
                for i in range(2):
                    for t in range(2):
                        last = exact(gen[i][:, t * D:(t + 1) * D],
                                     [(col(oT, k, (2 * i + t) * P, P), col(wo, k, 0, D)) for k in range(KD)])
                    last.then_inc(s["oproj"], 1)
                norm_t(b, 2)

                def gate_hidden(n):
                    c, j = n // KF, n % KF
                    need(pe, "a_", NCH, b, n - 1)
                    for i in range(2):
                        last = exact(big[:, n % 2, i * HALF:(i + 1) * HALF],
                                     [(col(wgh, k, i * F + j * P, P), col(hs, k, c * HALF, HALF)) for k in range(KD)])
                    last.then_inc(s["gh_mm"], 1)

                def down(n):
                    c, j = n // KF, n % KF
                    need(pe, "ah", NCH, b, n + 1)
                    need(pe, "a_lo", NCH, b, n + 1)
                    for t in range(2):
                        last = exact(gen[c][:, t * D:(t + 1) * D],
                                     [([p[:, n % 2, t * P:(t + 1) * P] for p in a2], [p[:, j, :] for p in wout])],
                                     start=(j == 0 and t == 0), stop=(j == KF - 1), skip_group_check=True)
                    last.then_inc(s["y_mm"], 1)

                gate_hidden(0)
                for n in range(NCH):
                    if n + 1 < NCH:
                        gate_hidden(n + 1)
                    down(n)

            sequence(0)
            with pe.Fori(1, B) as b:
                sequence(b)

            pe.wait_ge(s["x2_"], 2 * B)
            pe.wait_ge(s["wsum"], 1)
            pe.matmul(gen[0][:, 0:1], ones[:, :], wabs[:, :], start=True, stop=True).then_inc(s["wsum_mm"], 1)
            pe.wait_ge(s["tern"], 1)
            down_t = big[:, 0, :].bitcast(BF16)
            for j in range(KF):
                for r in range(KD):
                    last = pe.transpose(down_t[:, (j * KD + r) * P:(j * KD + r + 1) * P], tern[:, r * F + j * P:r * F + (j + 1) * P], ident_bf[:, :])
            last.then_inc(s["tern_t_"], 1)
            pe.wait_ge(s["raw_up_load"], 16)
            transpose_weights(WG_UP, "up_t", "up_lo")
            pe.wait_ge(s["up_lo"], len(WG_UP))
            pe.wait_ge(s["tern_c"], 1)

            def sequence_b(b):
                norm_t(b, 3)

                def unit(i):
                    t, c = i // 2, i % 2
                    for which, first, sem_, free in ((0, F, "g_mm", "gelu"), (1, 0, "v2_mm", "hmul")):
                        need(pe, free, 2 * TT, b, i - 1)
                        exact(big[:, which, i % 2 * S:i % 2 * S + S],
                              [(col(hs, k, t * P, P), col(wup, k, first + c * S, S)) for k in range(KD)]).then_inc(s[sem_], 1)

                def q_transpose(t):
                    need(pe, "qi_", TT, b, t + 1)
                    need(pe, "q_tc", TT, b, t - 1)
                    for j in range(KF):
                        last = pe.transpose(pvb[t % 2][:, :].bitcast(BF16)[:, j * P:(j + 1) * P], qi[t % 2][:, j * P:(j + 1) * P], ident_bf[:, :])
                    last.then_inc(s["q_t"], 1)

                def down(t):
                    need(pe, "q_tc", TT, b, t + 1)
                    need(pe, "final", TT, b, t - 1)
                    for j in range(KF):
                        last = pe.matmul(gen[t % 2][:, 0:D], qT[t % 2][:, j * P:(j + 1) * P], wdown[:, j, :], start=(j == 0), stop=(j == KF - 1))
                    last.then_inc(s["d_mm"], 1)

                unit(0)
                unit(1)
                for t in range(1, TT):
                    unit(2 * t)
                    unit(2 * t + 1)
                    q_transpose(t - 1)
                    down(t - 1)
                q_transpose(TT - 1)
                down(TT - 1)

            sequence_b(0)
            with pe.Fori(1, B) as b:
                sequence_b(b)


_L0 = ("attn_gamma_w", "attn_beta_w", "W_q", "W_k", "W_v", "W_o", "attn_alpha_w", "ffn_gamma_w", "ffn_beta_w",
       "gate_w", "hidden_w", "out_w", "out_b", "ffn_alpha_w")
_L1 = ("norm_w", "up_w", "down_w")
_INS = ["x", "cond_256"] + ["L0_cond_" + n for n in _L0] + ["L1_cond_" + n for n in _L1]


def kernel(**inputs):
    import numpy as _np
    import concourse.bacc as _bacc
    from concourse.bass_utils import run_bass_kernel_spmd as _run

    nc = _bacc.Bacc("TRN2", target_bir_lowering=False, num_devices=1)
    arrays, aps = {}, {}
    for name in _INS:
        a = _np.ascontiguousarray(inputs[name])
        arrays[f"in_{name}_dram"] = a
        aps[name] = nc.dram_tensor(f"in_{name}_dram", a.shape, mybir.dt.from_np(a.dtype), kind="ExternalInput").ap()
    out = nc.dram_tensor("out_dram", arrays["in_x_dram"].shape, F32, kind="ExternalOutput").ap()
    w = {n.split("_cond_")[1]: aps[n] for n in _INS[2:]}
    build(nc, aps["x"], aps["cond_256"], w, out)
    r = _run(nc, [arrays], core_ids=[0])
    return r.results[0]["out_dram"]
```

```python
from contextlib import ExitStack

import concourse.bass as bass
from concourse import mybir

F32 = mybir.dt.float32
F32R = mybir.dt.float32r
F16 = mybir.dt.float16
BF16 = mybir.dt.bfloat16
ALU = mybir.AluOpType
ACT = mybir.ActivationFunctionType
AX_X = mybir.AxisListType.X

P = 128
EPS = 1e-6
QUANT_EPS = 1e-5
ROUND = 12582912.0
P_SHIFT = 6.931471805599453


def build(nc, x, cond, w, out):
    B, S, D = x.shape
    C = cond.shape[1]
    F = w["gate_w"].shape[0]
    H = 16
    DH = D // H
    SCALE = (H / D) ** 0.5
    KD = D // P
    KF = F // P
    TT = S // P
    HT = P // DH
    NPART = 3
    KROWS = 6 * DH
    VW = NPART * DH + 1
    Q_PARTS = (0, 1, 2, 0, 1, 0)
    K_PARTS = (0, 0, 0, 1, 1, 2)
    NCH = 2 * KF
    HALF = S // 2

    STEPS = 2 * H
    LAG_ST = 11
    LAG_PV = LAG_ST + 3
    GROUP = 4
    Z_SQ1, Z_XN1, Z_H1, Z_QK, Z_V = 0, 1, 2, 3, 9
    Z_OT, Z_OL, Z_X1, Z_XN2, Z_H2 = 14, 15, 16, 17, 18
    Z_GH = [19 + n * 12 // NCH for n in range(NCH)]
    NP_BUF = 4
    ON_DVE = [m for m in range(STEPS) if m % 8 == 7]
    N_DVE = len(ON_DVE)
    N_POOL = STEPS - N_DVE

    KINDS = ("attn_gamma_w", "attn_beta_w", "ffn_gamma_w", "ffn_beta_w", "norm_w", "attn_alpha_w", "ffn_alpha_w")
    NSC = 5

    with ExitStack() as ctx:
        def sb(name, shape, dt=F32):
            return ctx.enter_context(nc.sbuf_tensor(name, shape, dt))

        def ps(name, shape, dt=F32):
            return ctx.enter_context(nc.psum_tensor(name, shape, dt))

        def sem(name):
            return ctx.enter_context(nc.semaphore(name))

        parts_d = nc.dram_tensor("parts_d", (B, 2, NPART, D, S), BF16).ap()
        v_d = nc.dram_tensor("v_d", (B, P, TT, H, VW), BF16).ap()
        shift_d = nc.dram_tensor("shift_d", (B, NPART, H * TT, P), BF16).ap()
        alpha_d = nc.dram_tensor("alpha_d", (B, 3 * D), F32).ap()
        x2_d = nc.dram_tensor("x2_d", (B, S, D), F32).ap()

        wqkv = [sb(f"wqkv{i}", [P, KD, 3 * D], F32R) for i in range(2)]
        wo = [sb(f"wo{i}", [P, KD, D], F32R) for i in range(2)]
        wgh = [sb(f"wgh{i}", [P, KD, 2 * F], F32R) for i in range(2)]
        wout = [sb(f"wout{i}", [P, KF, D], F32R) for i in range(2)]
        wup = wgh
        wdown = sb("wdown", [P, KF, D], BF16)
        ident = sb("ident", [P, P], F32)
        ident_bf = sb("ident_bf", [P, P], BF16)
        ones = sb("ones", [P, P], F32)
        half_pow = sb("half_pow", [P, TT], F32)
        condr = sb("condr", [B, C])
        condT = sb("condT", [C, B])
        p32 = sb("p32", [P, NP_BUF, 2 * S])
        p32_flat = p32[:, :, :].rearrange("p n t -> p (n t)")
        n_cw = len(KINDS) * KD * C
        cw = p32_flat[:, 0:n_cw].rearrange("p (n k c) -> p n k c", n=len(KINDS), k=KD)
        cwT = p32_flat[0:C, n_cw:n_cw + len(KINDS) * D].rearrange("c (n d) -> c n d", n=len(KINDS))
        table = sb("table", [P, NSC * KD, B])
        arow = sb("arow", [B, 3 * D])
        obrow = sb("obrow", [B, D])
        cur = sb("cur", [P, 2, NSC * KD])
        wabs = sb("wabs", [P, 1])
        wmean = sb("wmean", [P, 1])
        winv = sb("winv", [P, 1])
        wdeq = sb("wdeq", [P, 1])

        xa = sb("xa", [P, TT, D])
        xr = sb("xr", [P, TT, D])
        x1 = sb("x1", [P, TT, D])
        al = sb("al", [P, 3 * D])
        xn = sb("xn", [P, TT, D])
        stat = sb("stat", [P, 3, TT])
        h32 = sb("h32", [P, KD, S])
        hs = [sb(f"hs{i}", [P, KD, S], F32R) for i in range(2)]
        qk3 = sb("qk3", [P, 2, NPART, S], BF16)
        v3 = sb("v3", [P, TT, H, VW], BF16)
        qkres = h32
        qst = sb("qst", [P, H, S], BF16)
        kst = sb("kst", [P, H, S], BF16)
        vst = sb("vst", [P, TT, H, VW], BF16)
        negmax = sb("negmax", [P, H, TT])
        shift32 = sb("shift32", [GROUP * TT, 2, P])
        shift3 = sb("shift3", [GROUP * TT, NPART, P], BF16)
        ph = sb("ph", [P, NP_BUF, 2 * S], F16)
        pl = sb("pl", [P, NP_BUF, 2 * S], F16)
        osum = sb("osum", [P, 2 * TT, DH])
        orec = sb("orec", [P, 2 * TT])
        o = sb("o", [P, TT, D])
        oT = hs
        th = sb("th", [P, 2, HALF])
        ug = sb("ug", [P, 2, HALF])
        a32 = sb("a32", [P, 2, HALF])
        a2 = [sb(f"a2{i}", [P, 2, HALF], F32R) for i in range(2)]
        ge = p32
        hb = [qst[:, 4 * i:4 * i + 4, :].bitcast(F32).rearrange("p a b -> p (a b)") for i in range(2)]
        q32 = [qst[:, 8 + 4 * i:12 + 4 * i, :].bitcast(F32).rearrange("p a b -> p (a b)") for i in range(2)]
        qi = [kst[:, 2 * i:2 * i + 2, :].rearrange("p a b -> p (a b)") for i in range(2)]
        qT = [kst[:, 4 + 2 * i:6 + 2 * i, :].rearrange("p a b -> p (a b)") for i in range(2)]
        qs = sb("qs", [P, 2, 4])

        stage_q = qst[:, :, :].rearrange("p h t -> p (h t)").bitcast(F32)
        stage_k = kst[:, :, :].rearrange("p h t -> p (h t)").bitcast(F32)
        raw_qkvo = stage_q[:, 0:4 * KD * D].rearrange("p (n i) -> p n i", i=D)
        raw_out = stage_q[:, 4 * KD * D:4 * KD * D + KD * F].rearrange("p (n i) -> p n i", i=F)
        raw_gh = stage_k.rearrange("p (n i) -> p n i", i=D)
        raw_up = stage_q.rearrange("p (n i) -> p n i", i=D)
        raw_down = stage_k[:, 0:KD * F]
        tern_t = stage_k[:, KD * F:2 * KD * F]
        tern = tern_t.bitcast(BF16)[:, 0:KD * F]

        core = ps("core", [P, 4, 512])
        smb = [core[:, n, :] for n in range(2)]
        stb = [core[:, 2 + n, :] for n in range(2)]
        core_flat = core[:, :, :].rearrange("p a b -> p (a b)")
        pvb = ps("pvb", [P, 512])
        gen = [ps(f"gen{i}", [P, 512]) for i in range(3)]
        qtb = [pvb, gen[2]]
        QK_BANK, OT_BANK, OP_BANK = (2, 0, 1, 2), (2, 0), (1, 2)
        wbank = gen + [pvb]

        names = """past raw_load raw_up_load raw_down_load cond_load ob_load ident_set consts_set cond_t cond_tc cw_t cw_tc
        tab_mm tab_copy row_mm row_copy row_ob alpha_stored kones
        wt_t wt_hi wt_lo cur_set cur2_set
        xa_load xr_load al_load sq1 ms1 rs1 xn1 xt1 h32_1 hh1 hl1
        qk_mm qk_h qk_r qk_m qk_l v_mm v_h v_r v_m v_l parts0_st parts1_st v_st stack0_ld stack1_ld v0_ld v1_ld
        smax_mm smax shift_t shift_c shift_st shift_ld
        st_mm exp_ ph_ pl_pool pl_dve pv_mm o_sum o_rec o_norm
        o_t oh ol oproj xt_ x1_ x1b sq2 ms2 rs2 xn2 xt2 h32_2 hh2 hl2
        gh_mm tanh_ u_ a_ ah a_lo y_mm yt x2_ x2_st
        wsum wsum_mm wq_ tern tern_t_ tern_c up_t up_hi up_lo
        x2_ld sq3 ms3 rs3 xn3 xt3 h32_3 hh3 hl3 g_mm v2_mm gelu hmul amax qscale q32_ qi_ q_t q_tc d_mm final out_st
        """.split()
        s = {n: sem(n) for n in names}

        def need(eng, name, per, b, k):
            v = b * per + k
            if isinstance(v, int) and v <= 0:
                return
            eng.wait_ge(s[name], v)

        def past(eng, b):
            if not isinstance(b, int):
                eng.sem_inc(s["past"], 1)

        def need_low(eng, b, m):
            n = sum(k <= m % STEPS for k in ON_DVE)
            if m % STEPS in ON_DVE:
                need(eng, "pl_dve", N_DVE, b + m // STEPS, n)
            else:
                need(eng, "pl_pool", N_POOL, b + m // STEPS, m % STEPS + 1 - n)

        def run_pipeline(eng, iteration):
            for i in (-1, 0, 1):
                iteration(i, i >= 1, i >= 0, True)
            with eng.Fori(2, B - 1) as i:
                iteration(i, True, True, True)
            for i in (B - 1, B):
                iteration(i, True, i < B, False)

        def lagging(i, z, lag, prev, here):
            m = z - lag
            if m >= 0:
                return (i, m) if here else None
            return (i - 1, m + STEPS) if prev else None

        def groups(raw, rows, kchunks, dst):
            tiles = [(r, k) for k in range(kchunks) for r in range(rows)]
            return [([raw(r, k) for r, k in tiles[4 * g:4 * g + 4]],
                     [t[:, :, :].rearrange("p k n -> p (k n)")[:, 512 * g:512 * g + 512] for t in dst])
                    for g in range(len(tiles) // 4)]

        def cols(raw):
            return lambda r, k: raw[:, r, k * P:(k + 1) * P]

        WG = (groups(cols(raw_qkvo), 3 * KD, KD, wqkv)
              + groups(cols(raw_qkvo[:, 3 * KD:4 * KD, :]), KD, KD, wo)
              + groups(cols(raw_gh), 2 * KF, KD, wgh)
              + groups(cols(raw_out), KD, KF, wout))
        WG_UP = groups(cols(raw_up), 2 * KF, KD, wup)

        block = ctx.enter_context(nc.Block())

        def rows_of(t, b):
            return t[bass.ds(b, 1), :, :].rearrange("o (t p) d -> p (o t) d", p=P)

        @block.sync
        def _(sp):
            def need_sp(name, per, b, k):
                need(sp, name, per, b, k)
                past(sp, b)

            sp.dma_start(condr[:, :], cond).then_inc(s["cond_load"], 16)
            for i, n in enumerate(KINDS):
                sp.dma_start(cw[:, i, :, :], w[n].rearrange("(k p) c -> p k c", p=P)).then_inc(s["cond_load"], 16)
            sp.dma_start(obrow[:, :], w["out_b"].rearrange("(o d) -> o d", o=1).broadcast_to([B, D])).then_inc(s["ob_load"], 16)
            for i, n in enumerate(("W_q", "W_k", "W_v", "W_o")):
                sp.dma_start(raw_qkvo[:, KD * i:KD * i + KD, :], w[n].rearrange("(r p) i -> p r i", p=P)).then_inc(s["raw_load"], 16)
            for i, n in enumerate(("gate_w", "hidden_w")):
                sp.dma_start(raw_gh[:, KF * i:KF * i + KF, :], w[n].rearrange("(r p) i -> p r i", p=P)).then_inc(s["raw_load"], 16)
            sp.dma_start(raw_out, w["out_w"].rearrange("(r p) i -> p r i", p=P)).then_inc(s["raw_load"], 16)
            sp.wait_ge(s["row_ob"], 1)
            sp.dma_start(alpha_d, arow[:, :]).then_inc(s["alpha_stored"], 16)
            sp.wait_ge(s["alpha_stored"], 16)

            def stack(b, tile):
                for n in range(2):
                    need_sp(f"parts{n}_st", 16 * KD, b, 16 * KD)
                need_sp("st_mm", 2 * STEPS, b - 1, HT * 4 * (tile + 1))
                for st, which, parts in ((qst, 0, Q_PARTS), (kst, 1, K_PARTS)):
                    for g, part in enumerate(parts):
                        sp.dma_start(st[g * DH:(g + 1) * DH, tile * HT:(tile + 1) * HT, :],
                                     parts_d[bass.ds(b, 1), which, part, tile * P:(tile + 1) * P, :].rearrange("o (h d) t -> d (o h) t", d=DH)).then_inc(s[f"stack{tile}_ld"], 16)

            def v_load(b, tile):
                need_sp("v_st", 16, b, 16)
                need_sp("pv_mm", STEPS, b - 1, HT * 2 * (tile + 1))
                h0 = tile * HT
                sp.dma_start(vst[:, :, h0:h0 + HT, :],
                             v_d[bass.ds(b, 1), :, :, h0:h0 + HT, :].rearrange("o p t h w -> p (o t) (h w)")).then_inc(s[f"v{tile}_ld"], 16)

            def shift(b, g):
                n0, n1 = g * GROUP * TT, (g + 1) * GROUP * TT
                need_sp("shift_c", 5 * (H // GROUP), b, 5 * (g + 1))
                sp.dma_start(shift_d[bass.ds(b, 1), :, n0:n1, :].rearrange("o n m t -> m (o n) t"), shift3[:, :, :]).then_inc(s["shift_st"], 16)
                need_sp("shift_st", 16 * (H // GROUP), b, 16 * (g + 1))
                need_sp("st_mm", 2 * STEPS, b - 1, 4 * GROUP * (g + 1))
                sp.dma_start(qst[KROWS:KROWS + NPART, g * GROUP:(g + 1) * GROUP, :],
                             shift_d[bass.ds(b, 1), :, n0:n1, :].rearrange("o n (h j) t -> (o n) h (j t)", h=GROUP)).then_inc(s["shift_ld"], 16)

            def iteration(i, prev, here, prep):
                last, nxt = i - 1, i + 1
                if prep:
                    need_sp("sq1", TT, nxt, 0)
                    need_sp("xn1", TT, nxt, 0)
                    sp.dma_start(xa[:, :, :], rows_of(x, nxt)).then_inc(s["xa_load"], 16)
                if prev:
                    shift(last, H // GROUP - 1)
                    need_sp("x1_", 2, last, 0)
                    sp.dma_start(xr[:, :, :], rows_of(x, last)).then_inc(s["xr_load"], 16)
                    need_sp("yt", 2, last, 0)
                    need_sp("x1b", 1, last, 0)
                    sp.dma_start(al[:, :], alpha_d[bass.ds(last, 1), :].broadcast_to([P, 3 * D])).then_inc(s["al_load"], 16)
                if prep:
                    for j in range(2 * KD):
                        need_sp("qk_l", 2 * KD, nxt, j + 1)
                        sp.dma_start(parts_d[bass.ds(nxt, 1), j // KD, :, (j % KD) * P:(j % KD + 1) * P, :].rearrange("o n p t -> p (o n) t"),
                                     qk3[:, j % 2, :, :]).then_inc(s[f"parts{j % 2}_st"], 16)
                if here:
                    shift(i, 0)
                    stack(i, 1)
                if prep:
                    need_sp("v_l", TT, nxt, TT)
                    sp.dma_start(v_d[bass.ds(nxt, 1), :, :, :, :].rearrange("o p t h w -> p (o t h w)"), v3[:, :, :, :]).then_inc(s["v_st"], 16)
                if here:
                    v_load(i, 1)
                    shift(i, 1)
                    shift(i, 2)
                if prep:
                    if isinstance(i, int) and i == -1:
                        sp.wait_ge(s["wt_hi"], len(WG))
                        sp.wait_ge(s["wt_lo"], len(WG))
                    stack(nxt, 0)
                    v_load(nxt, 0)
                if prev:
                    need_sp("x2_", 2, last, 2)
                    sp.dma_start(rows_of(x2_d, last), x1[:, :, :]).then_inc(s["x2_st"], 16)

            run_pipeline(sp, iteration)

            sp.wait_ge(s["st_mm"], 2 * STEPS * B)
            sp.dma_start(raw_down.rearrange("p (r i) -> p r i", i=F), w["down_w"].rearrange("(r p) i -> p r i", p=P)).then_inc(s["raw_down_load"], 16)
            sp.dma_start(raw_up, w["up_w"].rearrange("(r p) i -> p r i", p=P)).then_inc(s["raw_up_load"], 16)
            sp.wait_ge(s["x2_st"], 16 * B)

            def sequence_b(b):
                need_sp("sq3", TT, b, 0)
                need_sp("xn3", TT, b, 0)
                sp.dma_start(xa[:, :, :], rows_of(x2_d, b)).then_inc(s["x2_ld"], 16)
                need_sp("final", TT, b, 0)
                sp.dma_start(xr[:, :, :], rows_of(x2_d, b)).then_inc(s["xr_load"], 16)
                need_sp("final", TT, b, TT)
                sp.dma_start(rows_of(out, b), x1[:, :, :]).then_inc(s["out_st"], 16)

            sequence_b(0)
            with sp.Fori(1, B) as b:
                sequence_b(b)
            sp.wait_ge(s["out_st"], 16 * B)

        @block.gpsimd
        def _(pool):
            pool.memset(ident[:, :], 0.0).then_inc(s["ident_set"], 1)
            pool.memset(ident_bf[:, :], 0.0).then_inc(s["ident_set"], 1)
            pool.wait_ge(s["ident_set"], 2)
            for m in (ident, ident_bf):
                pool.affine_select(out=m[:, :], in_=m[:, :], compare_op=ALU.not_equal, fill=1.0, base=0,
                                   pattern=[[-1, P]], channel_multiplier=1).then_inc(s["ident_set"], 1)
            pool.memset(ones[:, :], 1.0).then_inc(s["consts_set"], 1)
            pool.memset(half_pow[:, :], -0.5).then_inc(s["consts_set"], 1)
            pool.memset(v3[:, :, :, VW - 1:VW], 1.0).then_inc(s["consts_set"], 1)
            pool.wait_ge(s["consts_set"], 3)
            pool.wait_ge(s["wt_lo"], len(WG))
            pool.memset(kst[KROWS:KROWS + NPART, :, :], 1.0).then_inc(s["kones"], 1)
            pool.wait_ge(s["kones"], 1)

            def rstd(b, i):
                need(pool, f"sq{i}", TT, b, TT)
                past(pool, b)
                pool.tensor_scalar(stat[:, 1, :], stat[:, 0, :], 1.0 / D, EPS, ALU.mult, ALU.add).then_inc(s[f"ms{i}"], 1)
                need(pool, f"ms{i}", 1, b, 1)
                pool.tensor_tensor(stat[:, 2, :], stat[:, 1, :], half_pow[:, :], ALU.pow).then_inc(s[f"rs{i}"], 1)

            def h_lo(b, i):
                for k in range(KD):
                    need(pool, f"hh{i}", KD, b, k + 1)
                    pool.tensor_tensor(hs[1][:, k, :], h32[:, k, :], hs[0][:, k, :].bitcast(F32), ALU.subtract).then_inc(s[f"hl{i}"], 1)

            def low(b, m):
                need(pool, "ph_", STEPS, b, m + 1)
                need(pool, "pv_mm", STEPS, b, m + 1 - NP_BUF)
                pool.tensor_tensor(pl[:, m % NP_BUF, :], p32[:, m % NP_BUF, :], ph[:, m % NP_BUF, :], ALU.subtract).then_inc(s["pl_pool"], 1)

            def qk_parts(b, j):
                need(pool, "qk_r", 2 * KD, b, j + 1)
                past(pool, b)
                pool.tensor_scalar(qk3[:, j % 2, 1, :], qkres[:, j % 2, :], 1.0, 0.0, ALU.mult, ALU.add).then_inc(s["qk_m"], 1)
                need(pool, "qk_m", 2 * KD, b, j + 1)
                pool.tensor_tensor(qk3[:, j % 2, 2, :], qkres[:, j % 2, :], qk3[:, j % 2, 1, :], ALU.subtract).then_inc(s["qk_l"], 1)

            def v_parts(b, j):
                for t in (2 * j, 2 * j + 1):
                    need(pool, "v_r", TT // 2, b, j + 1)
                    past(pool, b)
                    res = qkres[:, j, :].rearrange("p (t h d) -> p t h d", t=2, h=H)[:, t % 2]
                    pool.tensor_scalar(v3[:, t, :, DH:2 * DH], res, 1.0, 0.0, ALU.mult, ALU.add).then_inc(s["v_m"], 1)
                    need(pool, "v_m", TT, b, t + 1)
                    pool.tensor_tensor(v3[:, t, :, 2 * DH:3 * DH], res, v3[:, t, :, DH:2 * DH], ALU.subtract).then_inc(s["v_l"], 1)

            def bias(b):
                need(pool, "xn2", TT, b, TT)
                need(pool, "al_load", 16, b, 16)
                pool.tensor_tensor(x1[:, :, :], x1[:, :, :], al[:, 2 * D:3 * D].unsqueeze(1).broadcast_to([P, TT, D]), ALU.add).then_inc(s["x1b"], 1)

            def a_low(b, n):
                need(pool, "ah", NCH, b, n + 1)
                need(pool, "y_mm", NCH, b, n - 1)
                pool.tensor_tensor(a2[1][:, n % 2, :], a32[:, n % 2, :], a2[0][:, n % 2, :].bitcast(F32), ALU.subtract).then_inc(s["a_lo"], 1)

            def iteration(i, prev, here, prep):
                last, nxt = i - 1, i + 1
                for z in range(STEPS):
                    if z - 1 >= 0 and (at := lagging(i, z - 1, LAG_ST, prev, here)) and at[1] not in ON_DVE:
                        low(*at)
                    if prep:
                        if z == Z_SQ1:
                            rstd(nxt, 1)
                        if z == Z_H1:
                            h_lo(nxt, 1)
                        if z - Z_QK - 1 in range(2 * KD):
                            qk_parts(nxt, z - Z_QK - 1)
                        if z - Z_V - 1 in range(TT // 2):
                            v_parts(nxt, z - Z_V - 1)
                    if prev:
                        if z == Z_X1:
                            rstd(last, 2)
                        if z == Z_XN2:
                            bias(last)
                        if z == Z_H2:
                            h_lo(last, 2)
                        for n in range(NCH):
                            if Z_GH[n] == z:
                                a_low(last, n)
                if (at := lagging(i, STEPS - 1, LAG_ST, prev, here)) and at[1] not in ON_DVE:
                    low(*at)

            run_pipeline(pool, iteration)

            def sequence_b(b):
                rstd(b, 3)
                need(pool, "v2_mm", 2 * TT, b, 0)
                h_lo(b, 3)
                for t in range(TT):
                    need(pool, "q32_", TT, b, t + 1)
                    need(pool, "q_t", TT, b, t - 1)
                    past(pool, b)
                    pool.tensor_scalar(qi[t % 2], q32[t % 2], -ROUND, 1.0, ALU.add, ALU.mult).then_inc(s["qi_"], 1)

            sequence_b(0)
            with pool.Fori(1, B) as b:
                sequence_b(b)

        @block.scalar
        def _(act):
            def split_hi(gs, t_sem, hi_sem, lo_sem):
                for g, (_, dst) in enumerate(gs):
                    act.wait_ge(s[t_sem], g + 1)
                    act.copy(dst[0], wbank[g % 4][:, :]).then_inc(s[hi_sem], 1)

            split_hi(WG, "wt_t", "wt_hi", "wt_lo")

            def squares(b, i, src):
                for t in range(TT):
                    act.activation(xn[:, t, :], src[:, t, :], ACT.Square, accum_out=stat[:, 0, t:t + 1]).then_inc(s[f"sq{i}"], 1)

            def h_hi(b, i):
                for k in range(KD):
                    need(act, f"h32_{i}", KD, b, k + 1)
                    act.copy(hs[0][:, k, :], h32[:, k, :]).then_inc(s[f"hh{i}"], 1)

            def exp(b, m):
                for k in range(2):
                    need(act, "st_mm", 2 * STEPS, b, 2 * m + k + 1)
                    if k == 0:
                        need_low(act, b, m - NP_BUF)
                    act.activation(p32[:, m % NP_BUF, k * S:(k + 1) * S], stb[k], ACT.Exp, scale=SCALE).then_inc(s["exp_"], 1)

            def high(b, m):
                need(act, "exp_", 2 * STEPS, b, 2 * m + 2)
                need(act, "pv_mm", STEPS, b, m + 1 - NP_BUF)
                act.copy(ph[:, m % NP_BUF, :], p32[:, m % NP_BUF, :]).then_inc(s["ph_"], 1)

            def tanh(b, n):
                need(act, "gh_mm", NCH, b, n + 1)
                need(act, "u_", NCH, b, n - 1)
                act.activation(th[:, n % 2, :], gen[n % 2][:, 0:HALF], ACT.Tanh, scale=0.5).then_inc(s["tanh_"], 1)

            def a_high(b, n):
                need(act, "a_", NCH, b, n + 1)
                need(act, "y_mm", NCH, b, n - 1)
                act.copy(a2[0][:, n % 2, :], a32[:, n % 2, :]).then_inc(s["ah"], 1)

            def iteration(i, prev, here, prep):
                last, nxt = i - 1, i + 1
                for z in range(STEPS):
                    if prep and z == Z_SQ1:
                        need(act, "xa_load", 16, nxt, 16)
                        squares(nxt, 1, xa)
                    if at := lagging(i, z, LAG_ST, prev, here):
                        exp(*at)
                    if at := lagging(i, z, LAG_ST + 1, prev, here):
                        high(*at)
                    if prep:
                        if z == Z_H1:
                            h_hi(nxt, 1)
                        if z - Z_QK in range(2 * KD):
                            j = z - Z_QK
                            need(act, "qk_mm", 2 * KD, nxt, j + 1)
                            need(act, f"parts{j % 2}_st", 16 * KD, nxt, 16 * (j // 2))
                            act.copy(qk3[:, j % 2, 0, :], gen[QK_BANK[j]][:, :]).then_inc(s["qk_h"], 1)
                        if z - Z_V in range(TT // 2):
                            j = z - Z_V
                            need(act, "v_mm", TT // 2, nxt, j + 1)
                            need(act, "v_st", 16, nxt, 0)
                            act.copy(v3[:, 2 * j:2 * j + 2, :, 0:DH], gen[j][:, :].rearrange("p (t h d) -> p t h d", t=2, h=H)).then_inc(s["v_h"], 1)
                    if prev:
                        if z == Z_OL:
                            for k in range(KD):
                                need(act, "o_t", KD, last, k + 1)
                                act.copy(hs[0][:, k, :], gen[OT_BANK[k]][:, :]).then_inc(s["oh"], 1)
                        if z == Z_X1:
                            need(act, "x1_", 2, last, 2)
                            squares(last, 2, x1)
                        if z == Z_H2:
                            h_hi(last, 2)
                        for n in range(NCH):
                            if Z_GH[n] == z:
                                tanh(last, n)
                                a_high(last, n)

            run_pipeline(act, iteration)

            split_hi(WG_UP, "up_t", "up_hi", "up_lo")

            def sequence_b(b):
                need(act, "x2_ld", 16, b, 16)
                squares(b, 3, xa)
                need(act, "v2_mm", 2 * TT, b, 0)
                h_hi(b, 3)
                for i in range(2 * TT):
                    need(act, "g_mm", 2 * TT, b, i + 1)
                    need(act, "hmul", 2 * TT, b, i - 1)
                    act.activation(ge[:, i % 2, 0:S], smb[i % 2], ACT.Gelu).then_inc(s["gelu"], 1)

            sequence_b(0)
            with act.Fori(1, B) as b:
                sequence_b(b)

        @block.vector
        def _(dve):
            dve.wait_ge(s["cond_t"], 1)
            dve.tensor_copy(condT[:, :], gen[0][0:C, 0:B]).then_inc(s["cond_tc"], 1)
            dve.wait_ge(s["cw_t"], 1)
            n_cwT = len(KINDS) * D
            dve.tensor_copy(p32_flat[0:C, n_cw:n_cw + n_cwT], core_flat[0:C, 0:n_cwT]).then_inc(s["cw_tc"], 1)
            dve.wait_ge(s["tab_mm"], 1)
            nt = NSC * KD
            dve.tensor_copy(table[:, 0:nt - KD, :].rearrange("p n b -> p (n b)"), gen[1][:, 0:(nt - KD) * B]).then_inc(s["tab_copy"], 1)
            dve.tensor_scalar(table[:, nt - KD:nt, :].rearrange("p n b -> p (n b)"), gen[1][:, (nt - KD) * B:nt * B], 1.0, None, ALU.add).then_inc(s["tab_copy"], 1)
            dve.wait_ge(s["row_mm"], 1)
            dve.tensor_copy(arow[:, 0:2 * D], pvb[0:B, :]).then_inc(s["row_copy"], 1)
            dve.wait_ge(s["row_copy"], 1)
            dve.wait_ge(s["ob_load"], 16)
            dve.tensor_tensor(arow[:, 2 * D:3 * D], arow[:, D:2 * D], obrow[:, :], ALU.mult).then_inc(s["row_ob"], 1)

            def split_lo(gs, hi_sem, lo_sem):
                for g, (_, dst) in enumerate(gs):
                    dve.wait_ge(s[hi_sem], g + 1)
                    dve.tensor_tensor(dst[1], wbank[g % 4][:, :], dst[0].bitcast(F32), ALU.subtract).then_inc(s[lo_sem], 1)

            split_lo(WG, "wt_hi", "wt_lo")
            dve.wait_ge(s["tab_copy"], 2)

            def xnorm(b, i, src):
                need(dve, f"rs{i}", 1, b, 1)
                for t in range(TT):
                    dve.tensor_scalar(xn[:, t, :], src[:, t, :], stat[:, 2, t:t + 1], None, ALU.mult).then_inc(s[f"xn{i}"], 1)

            def affine(b, i, gamma, beta, c):
                for k in range(KD):
                    need(dve, f"xt{i}", KD, b, k + 1)
                    scale = cur[:, c, gamma * KD + k:gamma * KD + k + 1]
                    if beta is None:
                        dve.tensor_scalar(h32[:, k, :], gen[k][:, :], scale, None, ALU.mult).then_inc(s[f"h32_{i}"], 1)
                    else:
                        dve.tensor_scalar(h32[:, k, :], gen[k][:, :], scale, cur[:, c, beta * KD + k:beta * KD + k + 1],
                                          ALU.mult, ALU.add).then_inc(s[f"h32_{i}"], 1)

            def two(t, i):
                return t[:, i, :].rearrange("p (t d) -> p t d", t=2)

            def scaled(b, i, name, src, col):
                dve.tensor_tensor(two(h32, i), src[:, :].rearrange("p (t d) -> p t d", t=2),
                                  al[:, col:col + D].unsqueeze(1).broadcast_to([P, 2, D]), ALU.mult).then_inc(s[name], 1)

            def maxima(b, n):
                need(dve, "smax_mm", 2 * STEPS, b, n + 1)
                dve.tensor_reduce(negmax[:, n // TT, n % TT:n % TT + 1], smb[n % 2], AX_X, ALU.max, negate=True).then_inc(s["smax"], 1)

            def shift_parts(b, g):
                ng = H // GROUP
                need(dve, "shift_t", ng, b, g + 1)
                dve.tensor_scalar(shift32[:, 0, :], smb[0][0:GROUP * TT, 0:P], P_SHIFT / SCALE, None, ALU.add).then_inc(s["shift_c"], 1)
                need(dve, "shift_st", 16 * ng, b, 16 * g)
                need(dve, "shift_c", 5 * ng, b, 5 * g + 1)
                dve.tensor_copy(shift3[:, 0, :], shift32[:, 0, :]).then_inc(s["shift_c"], 1)
                need(dve, "shift_c", 5 * ng, b, 5 * g + 2)
                dve.tensor_tensor(shift32[:, 1, :], shift32[:, 0, :], shift3[:, 0, :], ALU.subtract).then_inc(s["shift_c"], 1)
                need(dve, "shift_c", 5 * ng, b, 5 * g + 3)
                dve.tensor_copy(shift3[:, 1, :], shift32[:, 1, :]).then_inc(s["shift_c"], 1)
                need(dve, "shift_c", 5 * ng, b, 5 * g + 4)
                dve.tensor_tensor(shift3[:, 2, :], shift32[:, 1, :], shift3[:, 1, :], ALU.subtract).then_inc(s["shift_c"], 1)

            def low(b, m):
                need(dve, "ph_", STEPS, b, m + 1)
                need(dve, "pv_mm", STEPS, b, m + 1 - NP_BUF)
                dve.tensor_tensor(pl[:, m % NP_BUF, :], p32[:, m % NP_BUF, :], ph[:, m % NP_BUF, :], ALU.subtract).then_inc(s["pl_dve"], 1)

            def heads_out(b, r):
                need(dve, "pv_mm", STEPS, b, 4 * r + 4)
                need(dve, "o_norm", H, b, 2 * r)
                pv = pvb[:, 0:2 * TT * VW].rearrange("p (q w) -> p q w", w=VW)
                dve.tensor_reduce(osum[:, :, :], pv[:, :, 0:NPART * DH].rearrange("p q (n d) -> p q d n", n=NPART),
                                  AX_X, ALU.add).then_inc(s["o_sum"], 1)
                dve.reciprocal(orec[:, :].unsqueeze(2), pv[:, :, VW - 1:VW]).then_inc(s["o_rec"], 1)
                need(dve, "o_sum", H // 2, b, r + 1)
                need(dve, "o_rec", H // 2, b, r + 1)
                for k in range(2):
                    h = 2 * r + k
                    dve.tensor_tensor(o[:, :, h * DH:(h + 1) * DH], osum[:, k * TT:(k + 1) * TT, :],
                                      orec[:, k * TT:(k + 1) * TT].unsqueeze(2).broadcast_to([P, TT, DH]), ALU.mult).then_inc(s["o_norm"], 1)

            def qk_rest(b, j):
                need(dve, "qk_h", 2 * KD, b, j + 1)
                need(dve, "qk_l", 2 * KD, b, j - 1)
                dve.tensor_tensor(qkres[:, j % 2, :], gen[QK_BANK[j]][:, :], qk3[:, j % 2, 0, :], ALU.subtract).then_inc(s["qk_r"], 1)

            def v_rest(b, j):
                need(dve, "v_h", TT // 2, b, j + 1)
                need(dve, "qk_l", 2 * KD, b, 2 * KD - 1 + j)
                dve.tensor_tensor(qkres[:, j, :].rearrange("p (t h d) -> p t h d", t=2, h=H),
                                  gen[j][:, :].rearrange("p (t h d) -> p t h d", t=2, h=H),
                                  v3[:, 2 * j:2 * j + 2, :, 0:DH], ALU.subtract).then_inc(s["v_r"], 1)

            def swiglu(b, n):
                need(dve, "tanh_", NCH, b, n + 1)
                dve.scalar_tensor_tensor(out=ug[:, n % 2, :], in0=th[:, n % 2, :], scalar=1.0,
                                         in1=gen[n % 2][:, 0:HALF], op0=ALU.add, op1=ALU.mult).then_inc(s["u_"], 1)
                need(dve, "u_", NCH, b, n + 1)
                need(dve, "a_lo", NCH, b, n - 1)
                dve.scalar_tensor_tensor(out=a32[:, n % 2, :], in0=ug[:, n % 2, :], scalar=0.5,
                                         in1=gen[n % 2][:, HALF:2 * HALF], op0=ALU.mult, op1=ALU.mult).then_inc(s["a_"], 1)

            def second_residual(b, c):
                if c == 0:
                    need(dve, "x1b", 1, b, 1)
                need(dve, "y_mm", NCH, b, KF * (c + 1))
                scaled(b, c, "yt", gen[2], D)
                need(dve, "yt", 2, b, c + 1)
                dve.tensor_tensor(x1[:, 2 * c:2 * c + 2, :], two(h32, c), x1[:, 2 * c:2 * c + 2, :], ALU.add).then_inc(s["x2_"], 1)

            def iteration(i, prev, here, prep):
                last, nxt = i - 1, i + 1
                for z in range(STEPS):
                    if (at := lagging(i, z, LAG_PV + 1, prev, here)) and at[1] % 4 == 3:
                        heads_out(at[0], at[1] // 4)
                    if here and z > 0 and z % (2 * GROUP) == 0:
                        shift_parts(i, z // (2 * GROUP) - 1)
                    if prev and z == 0:
                        shift_parts(last, H // GROUP - 1)
                    if here:
                        maxima(i, 2 * z)
                        maxima(i, 2 * z + 1)
                    if (at := lagging(i, z, LAG_ST + 1, prev, here)) and at[1] in ON_DVE:
                        low(*at)
                    if prep:
                        if z == Z_XN1:
                            dve.tensor_copy(cur[:, 0, :].unsqueeze(2), table[:, :, bass.ds(nxt, 1)]).then_inc(s["cur_set"], 1)
                            xnorm(nxt, 1, xa)
                        if z == Z_H1:
                            need(dve, "cur_set", 1, nxt, 1)
                            affine(nxt, 1, 0, 1, 0)
                        if z - Z_QK - 1 in range(2 * KD):
                            qk_rest(nxt, z - Z_QK - 1)
                        if z - Z_V - 1 in range(TT // 2):
                            v_rest(nxt, z - Z_V - 1)
                    if prev:
                        if z == Z_OL:
                            for k in range(KD):
                                need(dve, "oh", KD, last, k + 1)
                                dve.tensor_tensor(hs[1][:, k, :], gen[OT_BANK[k]][:, :], hs[0][:, k, :].bitcast(F32), ALU.subtract).then_inc(s["ol"], 1)
                        if z == Z_X1:
                            need(dve, "al_load", 16, last, 16)
                            need(dve, "xr_load", 16, last, 16)
                            need(dve, "x2_st", 16, last, 0)
                            dve.tensor_copy(cur[:, 1, :].unsqueeze(2), table[:, :, bass.ds(last, 1)]).then_inc(s["cur2_set"], 1)
                            if prep:
                                need(dve, "v_l", TT, nxt, TT)
                            for c in range(2):
                                need(dve, "oproj", 2, last, c + 1)
                                scaled(last, c, "xt_", gen[OP_BANK[c]], 0)
                                need(dve, "xt_", 2, last, c + 1)
                                dve.tensor_tensor(x1[:, 2 * c:2 * c + 2, :], two(h32, c), xr[:, 2 * c:2 * c + 2, :], ALU.add).then_inc(s["x1_"], 1)
                        if z == Z_XN2:
                            xnorm(last, 2, x1)
                        if z == Z_H2:
                            need(dve, "cur2_set", 1, last, 1)
                            affine(last, 2, 2, 3, 1)
                        for n in range(NCH):
                            if Z_GH[n] == z:
                                swiglu(last, n)
                                if n == KF:
                                    second_residual(last, 0)
                if prev:
                    second_residual(last, 1)

            run_pipeline(dve, iteration)

            dve.wait_ge(s["raw_down_load"], 16)
            dve.tensor_reduce(wabs[:, :], raw_down, AX_X, ALU.add, apply_absolute_value=True).then_inc(s["wsum"], 1)
            dve.wait_ge(s["wsum_mm"], 1)
            dve.tensor_scalar(wmean[:, :], gen[0][:, 0:1], 1.0 / (D * F), QUANT_EPS, ALU.mult, ALU.max).then_inc(s["wq_"], 1)
            dve.wait_ge(s["wq_"], 1)
            dve.reciprocal(winv[:, :], wmean[:, :]).then_inc(s["wq_"], 1)
            dve.wait_ge(s["wq_"], 2)
            dve.tensor_scalar(tern_t, raw_down, winv[:, 0:1], 1.0, ALU.mult, ALU.min).then_inc(s["wq_"], 1)
            dve.wait_ge(s["wq_"], 3)
            dve.tensor_scalar(raw_down, tern_t, -1.0, ROUND, ALU.max, ALU.add).then_inc(s["wq_"], 1)
            dve.wait_ge(s["wq_"], 4)
            dve.tensor_scalar(tern, raw_down, ROUND, None, ALU.subtract).then_inc(s["tern"], 1)
            dve.wait_ge(s["tern_t_"], 1)
            dve.tensor_copy(wdown[:, :, :].rearrange("p k n -> p (k n)"), core_flat[:, 0:KD * P * KF // 2].bitcast(BF16)).then_inc(s["tern_c"], 1)
            split_lo(WG_UP, "up_hi", "up_lo")

            def sequence_b(b):
                dve.tensor_copy(cur[:, 0, :].unsqueeze(2), table[:, :, bass.ds(b, 1)]).then_inc(s["cur_set"], 1)
                xnorm(b, 3, xa)
                need(dve, "cur_set", 1, b + B, 1)
                affine(b, 3, 4, None, 0)

                def h_mul(i):
                    t, c = i // 2, i % 2
                    need(dve, "gelu", 2 * TT, b, i + 1)
                    need(dve, "v2_mm", 2 * TT, b, i + 1)
                    dve.tensor_tensor(hb[t % 2][:, c * S:(c + 1) * S], stb[i % 2], ge[:, i % 2, 0:S], ALU.mult).then_inc(s["hmul"], 1)

                def quantise(t):
                    need(dve, "hmul", 2 * TT, b, 2 * t + 2)
                    q = [qs[:, t % 2, n:n + 1] for n in range(4)]
                    dve.tensor_reduce(q[0], hb[t % 2], AX_X, ALU.max, apply_absolute_value=True).then_inc(s["amax"], 1)
                    need(dve, "amax", TT, b, t + 1)
                    dve.tensor_scalar(q[1], q[0], QUANT_EPS, 1.0 / 127.0, ALU.max, ALU.mult).then_inc(s["qscale"], 1)
                    need(dve, "qscale", 3 * TT, b, 3 * t + 1)
                    dve.reciprocal(q[2], q[1]).then_inc(s["qscale"], 1)
                    dve.tensor_scalar(q[3], q[1], wmean[:, 0:1], None, ALU.mult).then_inc(s["qscale"], 1)
                    need(dve, "qscale", 3 * TT, b, 3 * t + 3)
                    need(dve, "qi_", TT, b, t - 1)
                    dve.tensor_scalar(q32[t % 2], hb[t % 2], q[2], ROUND, ALU.mult, ALU.add).then_inc(s["q32_"], 1)

                def q_copy(t):
                    need(dve, "q_t", TT, b, t + 1)
                    need(dve, "d_mm", TT, b, t - 1)
                    dve.tensor_scalar(qT[t % 2], qtb[t % 2][:, :].bitcast(BF16), 127.0, -128.0, ALU.min, ALU.max).then_inc(s["q_tc"], 1)

                def finish(t):
                    need(dve, "d_mm", TT, b, t + 1)
                    dve.scalar_tensor_tensor(out=x1[:, t, :], in0=gen[t % 2][:, 0:D], scalar=qs[:, t % 2, 3:4],
                                             in1=xr[:, t, :], op0=ALU.mult, op1=ALU.add).then_inc(s["final"], 1)

                h_mul(0)
                h_mul(1)
                quantise(0)
                need(dve, "xr_load", 16, b + B, 16)
                need(dve, "out_st", 16, b, 0)
                for t in range(1, TT):
                    h_mul(2 * t)
                    h_mul(2 * t + 1)
                    q_copy(t - 1)
                    if t >= 2:
                        finish(t - 2)
                    quantise(t)
                q_copy(TT - 1)
                finish(TT - 2)
                finish(TT - 1)

            dve.wait_ge(s["x2_st"], 16 * B)
            sequence_b(0)
            with dve.Fori(1, B) as b:
                sequence_b(b)

        @block.tensor
        def _(pe):
            def exact(out_, terms, start=True, stop=True, **kw):
                passes = [(l[a], r[c]) for l, r in terms for a, c in ((0, 0), (0, 1), (1, 0))]
                for i, (l, r) in enumerate(passes):
                    last = pe.matmul(out_, l, r, start=start and i == 0, stop=stop and i == len(passes) - 1, **kw)
                return last

            pe.wait_ge(s["ident_set"], 4)
            pe.wait_ge(s["cond_load"], 16 * (1 + len(KINDS)))
            pe.transpose(gen[0][0:C, 0:B], condr[:, :], ident[0:B, 0:B]).then_inc(s["cond_t"], 1)
            for i in range(len(KINDS)):
                for k in range(KD):
                    last = pe.transpose(core_flat[0:C, (i * KD + k) * P:(i * KD + k + 1) * P], cw[:, i, k, :], ident[:, :])
            last.then_inc(s["cw_t"], 1)
            pe.wait_ge(s["cond_tc"], 1)
            pe.wait_ge(s["cw_tc"], 1)
            for i in range(NSC):
                for k in range(KD):
                    n = i * KD + k
                    last = pe.matmul(gen[1][:, n * B:(n + 1) * B], cwT[:, i, k * P:(k + 1) * P], condT[:, :], start=True, stop=True)
            last.then_inc(s["tab_mm"], 1)
            pe.matmul(pvb[0:B, :], condT[:, :], cwT[:, NSC:NSC + 2, :].rearrange("c n d -> c (n d)"), start=True, stop=True).then_inc(s["row_mm"], 1)
            pe.wait_ge(s["tab_copy"], 2)
            pe.wait_ge(s["row_copy"], 1)

            def transpose_weights(gs, t_sem, lo_sem):
                for g, (src, _) in enumerate(gs):
                    if g >= 4:
                        pe.wait_ge(s[lo_sem], g - 3)
                    for i, a in enumerate(src):
                        last = pe.transpose(wbank[g % 4][:, i * P:(i + 1) * P], a, ident[:, :])
                    last.then_inc(s[t_sem], 1)

            pe.wait_ge(s["raw_load"], 16 * 7)
            transpose_weights(WG, "wt_t", "wt_lo")
            pe.wait_ge(s["wt_lo"], len(WG))
            pe.wait_ge(s["consts_set"], 3)

            def norm_t(b, i):
                need(pe, f"xn{i}", TT, b, TT)
                for k in range(KD):
                    for t in range(TT):
                        last = pe.transpose(gen[k][:, t * P:(t + 1) * P], xn[:, t, k * P:(k + 1) * P], ident[:, :])
                    last.then_inc(s[f"xt{i}"], 1)

            def col(pair, k, a, n):
                return [t[:, k, a:a + n] for t in pair]

            def scores_max(b, n):
                if n % (2 * TT * HT // 2) == 0:
                    tile = n // (TT * HT)
                    need(pe, f"stack{tile}_ld", 192, b, 192)
                need(pe, "smax", 2 * STEPS, b, n - 1)
                h, q = n // TT, n % TT
                pe.matmul(smb[n % 2], qst[0:KROWS, h, q * P:(q + 1) * P], kst[0:KROWS, h, :], start=True, stop=True).then_inc(s["smax_mm"], 1)

            def shift_turn(b, g):
                need(pe, "smax", 2 * STEPS, b, TT * GROUP * (g + 1))
                pe.transpose(smb[0][0:GROUP * TT, 0:P], negmax[:, g * GROUP:(g + 1) * GROUP, :].rearrange("p h t -> p (h t)"), ident[:, :]).then_inc(s["shift_t"], 1)

            def scores(b, m):
                h = m // 2
                if m % (2 * GROUP) == 0:
                    need(pe, "shift_ld", 16 * (H // GROUP), b, 16 * (m // (2 * GROUP) + 1))
                for k in range(2):
                    need(pe, "exp_", 2 * STEPS, b, 2 * m + k - 1)
                    k0 = (2 * (m % 2) + k) * P
                    last = pe.matmul(stb[k], kst[0:KROWS + NPART, h, k0:k0 + P], qst[0:KROWS + NPART, h, :], start=True, stop=True)
                    last.then_inc(s["st_mm"], 1)

            def weighted(b, m):
                h = m // 2
                if m % (2 * HT) == 0:
                    need(pe, f"v{m // (2 * HT)}_ld", 16, b, 16)
                if m % 4 == 0:
                    need(pe, "o_rec", H // 2, b, h // 2)
                need(pe, "ph_", STEPS, b, m + 1)
                need_low(pe, b, m)
                for q in range(TT):
                    for k in range(2):
                        for part in (ph, pl):
                            a, w0 = k * S + q * P, ((h % 2) * TT + q) * VW
                            last = pe.matmul(pvb[:, w0:w0 + VW], part[:, m % NP_BUF, a:a + P], vst[:, 2 * (m % 2) + k, h, :],
                                             start=(m % 4 == 0 and q == 0 and k == 0 and part is ph),
                                             stop=(m % 2 == 1 and k == 1 and part is pl), skip_group_check=True)
                last.then_inc(s["pv_mm"], 1)

            def project_qk(b, j):
                if j == 3:
                    need(pe, "qk_r", 2 * KD, b, 1)
                exact(gen[QK_BANK[j]][:, :], [(col(wqkv, k, j * P, P), col(hs, k, 0, S)) for k in range(KD)]).then_inc(s["qk_mm"], 1)

            def project_v(b, j):
                need(pe, "qk_r", 2 * KD, b, 2 + j)
                for t in range(2):
                    last = exact(gen[j][:, t * D:(t + 1) * D],
                                 [(col(hs, k, (2 * j + t) * P, P), col(wqkv, k, 2 * D, D)) for k in range(KD)])
                last.then_inc(s["v_mm"], 1)

            def turn_o(b, prep):
                need(pe, "o_norm", H, b, H)
                if prep is not None:
                    need(pe, "qk_r", 2 * KD, prep, 2 * KD)
                    need(pe, "v_r", TT // 2, prep, TT // 2)
                for k in range(KD):
                    for t in range(TT):
                        last = pe.transpose(gen[OT_BANK[k]][:, t * P:(t + 1) * P], o[:, t, k * P:(k + 1) * P], ident[:, :])
                    last.then_inc(s["o_t"], 1)

            def project_o(b):
                need(pe, "oh", KD, b, KD)
                need(pe, "ol", KD, b, KD)
                for c in range(2):
                    for t in range(2):
                        last = exact(gen[OP_BANK[c]][:, t * D:(t + 1) * D],
                                     [(col(oT, k, (2 * c + t) * P, P), col(wo, k, 0, D)) for k in range(KD)])
                    last.then_inc(s["oproj"], 1)

            def gate_hidden(b, n):
                c, j = n // KF, n % KF
                if n == 0:
                    need(pe, "hh2", KD, b, KD)
                    need(pe, "hl2", KD, b, KD)
                need(pe, "a_", NCH, b, n - 1)
                for k2 in range(2):
                    last = exact(gen[n % 2][:, k2 * HALF:(k2 + 1) * HALF],
                                 [(col(wgh, k, k2 * F + j * P, P), col(hs, k, c * HALF, HALF)) for k in range(KD)])
                last.then_inc(s["gh_mm"], 1)

            def swiglu_down(b, n):
                c, j = n // KF, n % KF
                if n == KF:
                    need(pe, "yt", 2, b, 1)
                need(pe, "ah", NCH, b, n + 1)
                need(pe, "a_lo", NCH, b, n + 1)
                for t in range(2):
                    last = exact(gen[2][:, t * D:(t + 1) * D],
                                 [([p[:, n % 2, t * P:(t + 1) * P] for p in a2], [p[:, j, :] for p in wout])],
                                 start=(j == 0 and t == 0), stop=(j == KF - 1), skip_group_check=True)
                last.then_inc(s["y_mm"], 1)

            def iteration(i, prev, here, prep):
                last, nxt = i - 1, i + 1
                for z in range(STEPS):
                    if here and z > 0 and z % (2 * GROUP) == 0:
                        shift_turn(i, z // (2 * GROUP) - 1)
                    if prev and z == 0:
                        shift_turn(last, H // GROUP - 1)
                    if here:
                        if z % (2 * GROUP) == 0 and (prev or z > 0):
                            b, g = (i, z // (2 * GROUP) - 1) if z else (last, H // GROUP - 1)
                            need(pe, "shift_c", 5 * (H // GROUP), b, 5 * g + 1)
                        scores_max(i, 2 * z)
                        scores_max(i, 2 * z + 1)
                    if at := lagging(i, z, LAG_ST, prev, here):
                        if isinstance(i, int) and i == 0:
                            pe.wait_ge(s["kones"], 1)
                        scores(*at)
                    if prep:
                        if z == Z_XN1:
                            norm_t(nxt, 1)
                        if z == Z_QK:
                            need(pe, "hh1", KD, nxt, KD)
                            need(pe, "hl1", KD, nxt, KD)
                        if z - Z_QK in range(2 * KD):
                            project_qk(nxt, z - Z_QK)
                        if z - Z_V in range(TT // 2):
                            project_v(nxt, z - Z_V)
                    if prev:
                        if z == Z_OT:
                            turn_o(last, nxt if prep else None)
                        if z == Z_OL:
                            project_o(last)
                        if z == Z_XN2:
                            norm_t(last, 2)
                        for n in range(NCH):
                            if Z_GH[n] == z:
                                gate_hidden(last, n)
                                if n >= 1:
                                    swiglu_down(last, n - 1)
                    if at := lagging(i, z, LAG_PV, prev, here):
                        weighted(*at)
                if prev:
                    swiglu_down(last, NCH - 1)

            run_pipeline(pe, iteration)

            pe.wait_ge(s["x2_"], 2 * B)
            pe.wait_ge(s["wsum"], 1)
            pe.matmul(gen[0][:, 0:1], ones[:, :], wabs[:, :], start=True, stop=True).then_inc(s["wsum_mm"], 1)
            pe.wait_ge(s["tern"], 1)
            down_t = core_flat[:, 0:KD * P * KF // 2].bitcast(BF16)
            for j in range(KF):
                for r in range(KD):
                    last = pe.transpose(down_t[:, (j * KD + r) * P:(j * KD + r + 1) * P], tern[:, r * F + j * P:r * F + (j + 1) * P], ident_bf[:, :])
            last.then_inc(s["tern_t_"], 1)
            pe.wait_ge(s["raw_up_load"], 16)
            transpose_weights(WG_UP, "up_t", "up_lo")
            pe.wait_ge(s["up_lo"], len(WG_UP))
            pe.wait_ge(s["tern_c"], 1)

            def sequence_b(b):
                norm_t(b, 3)
                need(pe, "hh3", KD, b, KD)
                need(pe, "hl3", KD, b, KD)

                def unit(i):
                    t, c = i // 2, i % 2
                    for which, first, sem_, free in ((0, F, "g_mm", "gelu"), (1, 0, "v2_mm", "hmul")):
                        need(pe, free, 2 * TT, b, i - 1)
                        exact((smb, stb)[which][i % 2],
                              [(col(hs, k, t * P, P), col(wup, k, first + c * S, S)) for k in range(KD)]).then_inc(s[sem_], 1)

                def q_transpose(t):
                    need(pe, "qi_", TT, b, t + 1)
                    need(pe, "q_tc", TT, b, t - 1)
                    for j in range(KF):
                        last = pe.transpose(qtb[t % 2][:, :].bitcast(BF16)[:, j * P:(j + 1) * P], qi[t % 2][:, j * P:(j + 1) * P], ident_bf[:, :])
                    last.then_inc(s["q_t"], 1)

                def down(t):
                    need(pe, "q_tc", TT, b, t + 1)
                    need(pe, "final", TT, b, t - 1)
                    for j in range(KF):
                        last = pe.matmul(gen[t % 2][:, 0:D], qT[t % 2][:, j * P:(j + 1) * P], wdown[:, j, :], start=(j == 0), stop=(j == KF - 1))
                    last.then_inc(s["d_mm"], 1)

                unit(0)
                unit(1)
                for t in range(1, TT):
                    unit(2 * t)
                    unit(2 * t + 1)
                    q_transpose(t - 1)
                    down(t - 1)
                q_transpose(TT - 1)
                down(TT - 1)

            sequence_b(0)
            with pe.Fori(1, B) as b:
                sequence_b(b)


_L0 = ("attn_gamma_w", "attn_beta_w", "W_q", "W_k", "W_v", "W_o", "attn_alpha_w", "ffn_gamma_w", "ffn_beta_w",
       "gate_w", "hidden_w", "out_w", "out_b", "ffn_alpha_w")
_L1 = ("norm_w", "up_w", "down_w")
_INS = ["x", "cond_256"] + ["L0_cond_" + n for n in _L0] + ["L1_cond_" + n for n in _L1]


def kernel(**inputs):
    import numpy as _np
    import concourse.bacc as _bacc
    from concourse.bass_utils import run_bass_kernel_spmd as _run

    nc = _bacc.Bacc("TRN2", target_bir_lowering=False, num_devices=1)
    arrays, aps = {}, {}
    for name in _INS:
        a = _np.ascontiguousarray(inputs[name])
        arrays[f"in_{name}_dram"] = a
        aps[name] = nc.dram_tensor(f"in_{name}_dram", a.shape, mybir.dt.from_np(a.dtype), kind="ExternalInput").ap()
    out = nc.dram_tensor("out_dram", arrays["in_x_dram"].shape, F32, kind="ExternalOutput").ap()
    w = {n.split("_cond_")[1]: aps[n] for n in _INS[2:]}
    build(nc, aps["x"], aps["cond_256"], w, out)
    r = _run(nc, [arrays], core_ids=[0])
    return r.results[0]["out_dram"]
```

```python
from contextlib import ExitStack

import concourse.bass as bass
from concourse import mybir

F32 = mybir.dt.float32
F32R = mybir.dt.float32r
F16 = mybir.dt.float16
BF16 = mybir.dt.bfloat16
ALU = mybir.AluOpType
ACT = mybir.ActivationFunctionType
AX_X = mybir.AxisListType.X

P = 128
EPS = 1e-6
QUANT_EPS = 1e-5
ROUND = 12582912.0
P_SHIFT = 6.931471805599453


def build(nc, x, cond, w, out):
    B, S, D = x.shape
    C = cond.shape[1]
    F = w["gate_w"].shape[0]
    H = 16
    DH = D // H
    SCALE = (H / D) ** 0.5
    KD = D // P
    KF = F // P
    TT = S // P
    HT = P // DH
    NPART = 3
    KROWS = 6 * DH
    VW = NPART * DH + 1
    Q_PARTS = (0, 1, 2, 0, 1, 0)
    K_PARTS = (0, 0, 0, 1, 1, 2)
    NCH = 2 * KF
    HALF = S // 2

    STEPS = 2 * H
    T_SQ1, T_XN1, T_XT1, T_H1, T_HH1, T_HL1 = 1, 2, 3, 4, 5, 5
    T_QK, T_V = (7, 8, 10, 11), (12, 13)
    T_MAX = 18
    GROUP = 4
    T_TURN = [T_MAX + 2 * GROUP * (g + 1) for g in range(H // GROUP)]
    T_ST = T_MAX + 11
    T_PV = T_ST + 3
    T_OT = T_PV + STEPS + 1
    T_OP = (T_OT + 3, T_OT + 4)
    T_SQ2, T_XN2, T_XT2, T_H2, T_HH2, T_HL2 = [T_OT + n for n in (6, 7, 8, 9, 10, 10)]
    T_GH = [T_OT + 13 + n - (n > 5) for n in range(NCH)]
    T_DOWN = [t + 2 for t in T_GH]
    T_BIAS = T_OT + 17
    Z_TERN = 4
    assert T_DOWN[-1] + 1 < 3 * STEPS
    NP_BUF = 4
    ON_DVE = [6, 8, 10, 12, 14]
    N_DVE = len(ON_DVE)
    N_POOL = STEPS - N_DVE

    KINDS = ("attn_gamma_w", "attn_beta_w", "ffn_gamma_w", "ffn_beta_w", "norm_w", "attn_alpha_w", "ffn_alpha_w")
    NSC = 5

    with ExitStack() as ctx:
        def sb(name, shape, dt=F32):
            return ctx.enter_context(nc.sbuf_tensor(name, shape, dt))

        def ps(name, shape, dt=F32):
            return ctx.enter_context(nc.psum_tensor(name, shape, dt))

        def sem(name):
            return ctx.enter_context(nc.semaphore(name))

        parts_d = nc.dram_tensor("parts_d", (B, 2, NPART, D, S), BF16).ap()
        v_d = nc.dram_tensor("v_d", (B, P, TT, H, VW), BF16).ap()
        shift_d = nc.dram_tensor("shift_d", (B, NPART, H * TT, P), BF16).ap()
        alpha_d = nc.dram_tensor("alpha_d", (B, 3 * D), F32).ap()
        x2_d = nc.dram_tensor("x2_d", (B, S, D), F32).ap()

        wqkv = [sb(f"wqkv{i}", [P, KD, 3 * D], F32R) for i in range(2)]
        wo = [sb(f"wo{i}", [P, KD, D], F32R) for i in range(2)]
        wgh = [sb(f"wgh{i}", [P, KD, 2 * F], F32R) for i in range(2)]
        wout = [sb(f"wout{i}", [P, KF, D], F32R) for i in range(2)]
        wup = wgh
        ident = sb("ident", [P, P], F32)
        ident_bf = sb("ident_bf", [P, P], BF16)
        ones = sb("ones", [P, P], F32)
        half_pow = sb("half_pow", [P, TT], F32)
        condr = sb("condr", [B, C])
        condT = sb("condT", [C, B])
        p32 = sb("p32", [P, NP_BUF, 2 * S])
        p32_flat = p32[:, :, :].rearrange("p n t -> p (n t)")
        n_cw = len(KINDS) * KD * C
        cw = p32_flat[:, 0:n_cw].rearrange("p (n k c) -> p n k c", n=len(KINDS), k=KD)
        cwT = p32_flat[0:C, n_cw:n_cw + len(KINDS) * D].rearrange("c (n d) -> c n d", n=len(KINDS))
        table = sb("table", [P, NSC * KD, B])
        cur = sb("cur", [P, 2, NSC * KD])
        wabs = sb("wabs", [P, 1])
        wmean = sb("wmean", [P, 1])
        winv = sb("winv", [P, 1])
        wdeq = sb("wdeq", [P, 1])

        xa = sb("xa", [P, TT, D])
        xr = sb("xr", [P, TT, D])
        x1 = sb("x1", [P, TT, D])
        al = sb("al", [P, 3 * D])
        arow = al[0:B, :]
        obrow = xr[0:B, 0, :]
        xn = sb("xn", [P, TT, D])
        stat = sb("stat", [P, 2, 3, TT])
        h32 = sb("h32", [P, KD, S])
        hp = [sb(f"hp{i}", [P, KD, S], F32R) for i in range(2)]
        hs = [sb(f"hs{i}", [P, KD, S], F32R) for i in range(2)]
        qk3 = sb("qk3", [P, 2, NPART, S], BF16)
        v3 = sb("v3", [P, TT, H, VW], BF16)
        qst = sb("qst", [P, H, S], BF16)
        kst = sb("kst", [P, H, S], BF16)
        vst = sb("vst", [P, TT, H, VW], BF16)
        negmax = sb("negmax", [P, H, TT])
        shift32 = sb("shift32", [GROUP * TT, 2, P])
        shift3 = sb("shift3", [GROUP * TT, NPART, P], BF16)
        ph = sb("ph", [P, NP_BUF, 2 * S], F16)
        pl = sb("pl", [P, NP_BUF, 2 * S], F16)
        osum = sb("osum", [P, 2 * TT, DH])
        orec = sb("orec", [P, 2 * TT])
        o = sb("o", [P, TT, D])
        oT = hs
        th = sb("th", [P, 2, HALF])
        ug = sb("ug", [P, 2, HALF])
        xt = [t[:, :, :].rearrange("p n t -> p (n t)") for t in (th, ug)]
        xn_flat = xn[:, :, :].rearrange("p t d -> p (t d)")
        rest = xt + [xn_flat[:, 0:S], xn_flat[:, S:2 * S]]
        a32 = sb("a32", [P, 2, HALF])
        a2 = [sb(f"a2{i}", [P, 2, HALF], F32R) for i in range(2)]
        wdown = vst[:, :, :, :].rearrange("p t h w -> p (t h w)")[:, 0:KF * D].rearrange("p (k n) -> p k n", n=D)
        ge = p32
        hb = [qst[:, 4 * i:4 * i + 4, :].bitcast(F32).rearrange("p a b -> p (a b)") for i in range(2)]
        q32 = [qst[:, 8 + 4 * i:12 + 4 * i, :].bitcast(F32).rearrange("p a b -> p (a b)") for i in range(2)]
        qi = [kst[:, 2 * i:2 * i + 2, :].rearrange("p a b -> p (a b)") for i in range(2)]
        qT = [kst[:, 4 + 2 * i:6 + 2 * i, :].rearrange("p a b -> p (a b)") for i in range(2)]
        qs = sb("qs", [P, TT, 4])

        stage_q = qst[:, :, :].rearrange("p h t -> p (h t)").bitcast(F32)
        stage_k = kst[:, :, :].rearrange("p h t -> p (h t)").bitcast(F32)
        raw_qkvo = stage_q[:, 0:4 * KD * D].rearrange("p (n i) -> p n i", i=D)
        raw_out = stage_q[:, 4 * KD * D:4 * KD * D + KD * F].rearrange("p (n i) -> p n i", i=F)
        raw_gh = stage_k.rearrange("p (n i) -> p n i", i=D)
        raw_up = stage_q.rearrange("p (n i) -> p n i", i=D)
        raw_down = stage_k[:, 0:KD * F]
        tern_t = stage_k[:, KD * F:2 * KD * F]
        tern = tern_t.bitcast(BF16)[:, 0:KD * F]

        core = ps("core", [P, 4, 512])
        smb = [core[:, n, :] for n in range(2)]
        stb = [core[:, 2 + n, :] for n in range(2)]
        core_flat = core[:, :, :].rearrange("p a b -> p (a b)")
        pvb = ps("pvb", [P, 512])
        gen = [ps(f"gen{i}", [P, 512]) for i in range(3)]
        xt_bank = gen[0][:, 0:KD * P]
        down_bank = gen[1][:, 0:D]
        qt_bank = pvb[:, :].bitcast(BF16)
        XT_BANK, QK_BANK, V_BANK, OT_BANK, OP_BANK = (2, 0), (0, 1, 1, 2), (0, 2), (0, 1), (1, 2)
        Y_BANK = 2
        wbank = gen + [pvb]

        names = """past raw_ffn_load raw_up_load raw_down_load raw_qkvo_load cond_load ob_load ident_set consts_set cond_t cond_tc cw_t cw_tc
        tab_mm tab_copy row_mm row_copy row_ob alpha_stored kones
        wt_t wt_hi wt_lo cur_set cur2_set
        xa_load xr_load al_load sq1 ms1 rs1 xn1 xt1 h32_1 hh1 hl1
        qk_mm qk_h qk_r qk_m qk_l v_mm v_h v_r v_m v_l parts0_st parts1_st v_st stack0_ld stack1_ld v0_ld v1_ld
        smax_mm smax shift_t shift_c shift_st shift_ld
        st_mm exp_ ph_ pl_pool pl_dve pv_mm o_sum o_rec o_norm
        o_t oh ol oproj xt_ x1_ x1b sq2 ms2 rs2 xn2 xt2 h32_2 hh2 hl2
        gh_mm tanh_ u_ a_ ah a_lo y_mm yt x2_ x2_st
        wsum wsum_mm wq_ tern tern_t_ tern_c up_t up_hi up_lo
        x2_ld0 x2_ld1 x2_ld2 x2_ld3 xr_ld0 xr_ld1 xr_ld2 xr_ld3 out_st0 out_st1 out_st2 out_st3
        sq3 ms3 rs3 xn3 xt3 h32_3 hh3 hl3 g_mm v2_mm gelu hmul amax qscale q32_ qi_ q_t q_tc d_mm final
        """.split()
        s = {n: sem(n) for n in names}

        def need(eng, name, per, b, k):
            v = b * per + k
            if isinstance(v, int) and (v <= 0 or b >= B):
                return
            eng.wait_ge(s[name], v)

        def past(eng, b):
            if not isinstance(b, int):
                eng.sem_inc(s["past"], 1)

        def need_low(eng, b, m):
            n = sum(k <= m % STEPS for k in ON_DVE)
            if m % STEPS in ON_DVE:
                need(eng, "pl_dve", N_DVE, b + m // STEPS, n)
            else:
                need(eng, "pl_pool", N_POOL, b + m // STEPS, m % STEPS + 1 - n)

        def run_pipeline(eng, iteration):
            for i in (-1, 0, 1):
                iteration(i, i >= 1, i >= 0, True)
            with eng.Fori(2, B - 1) as i:
                iteration(i, True, True, True)
            for i in (B - 1, B):
                iteration(i, True, i < B, False)

        def timeline(i, prev, here, prep):
            there = (prep, here, prev)

            def at(z, t):
                return [i + 1 - t // STEPS] if t % STEPS == z and there[t // STEPS] else []

            def stream(z, t0):
                third = next(n for n in range(3) if t0 <= z + n * STEPS < t0 + STEPS)
                return [(i + 1 - third, z + third * STEPS - t0)] if there[third] else []

            return at, stream

        L_SQ3, L_XN3, L_XT3, L_H3, L_HH3 = -3, -2, -2, -1, -1
        L_Q, L_QT, L_DOWN = 0, 1, 2

        def tiles_at(i, prev, here, nxt):
            def at(z, lag):
                n = (z - lag) // TT
                return [(i + n, (z - lag) % TT)] if (here, nxt, prev)[n] else []

            return at

        def groups(raw, rows, kchunks, dst):
            tiles = [(r, k) for k in range(kchunks) for r in range(rows)]
            return [([raw(r, k) for r, k in tiles[4 * g:4 * g + 4]],
                     [t[:, :, :].rearrange("p k n -> p (k n)")[:, 512 * g:512 * g + 512] for t in dst])
                    for g in range(len(tiles) // 4)]

        def cols(raw):
            return lambda r, k: raw[:, r, k * P:(k + 1) * P]

        WG = (groups(cols(raw_qkvo), 3 * KD, KD, wqkv)
              + groups(cols(raw_qkvo[:, 3 * KD:4 * KD, :]), KD, KD, wo)
              + groups(cols(raw_gh), 2 * KF, KD, wgh)
              + groups(cols(raw_out), KD, KF, wout))
        WG_UP = groups(cols(raw_up), 2 * KF, KD, wup)

        block = ctx.enter_context(nc.Block())

        def rows_of(t, b):
            return t[bass.ds(b, 1), :, :].rearrange("o (t p) d -> p (o t) d", p=P)

        @block.sync
        def _(sp):
            def need_sp(name, per, b, k):
                need(sp, name, per, b, k)
                past(sp, b)

            sp.dma_start(condr[:, :], cond).then_inc(s["cond_load"], 16)
            for i, n in enumerate(KINDS):
                sp.dma_start(cw[:, i, :, :], w[n].rearrange("(k p) c -> p k c", p=P)).then_inc(s["cond_load"], 16)
            sp.dma_start(obrow[:, :], w["out_b"].rearrange("(o d) -> o d", o=1).broadcast_to([B, D])).then_inc(s["ob_load"], 16)
            for i, n in enumerate(("W_q", "W_k", "W_v", "W_o")):
                sp.dma_start(raw_qkvo[:, KD * i:KD * i + KD, :], w[n].rearrange("(r p) i -> p r i", p=P)).then_inc(s["raw_qkvo_load"], 16)
            for i, n in enumerate(("gate_w", "hidden_w")):
                sp.dma_start(raw_gh[:, KF * i:KF * i + KF, :], w[n].rearrange("(r p) i -> p r i", p=P)).then_inc(s["raw_ffn_load"], 16)
            sp.dma_start(raw_out, w["out_w"].rearrange("(r p) i -> p r i", p=P)).then_inc(s["raw_ffn_load"], 16)
            sp.wait_ge(s["row_ob"], 1)
            sp.dma_start(alpha_d, arow[:, :]).then_inc(s["alpha_stored"], 16)
            sp.wait_ge(s["alpha_stored"], 16)

            def stack(b, tile):
                for n in range(2):
                    need_sp(f"parts{n}_st", 16 * KD, b, 16 * (tile + 1))
                need_sp("st_mm", 2 * STEPS, b - 1, HT * 4 * (tile + 1))
                for st, which, parts in ((qst, 0, Q_PARTS), (kst, 1, K_PARTS)):
                    for g, part in enumerate(parts):
                        sp.dma_start(st[g * DH:(g + 1) * DH, tile * HT:(tile + 1) * HT, :],
                                     parts_d[bass.ds(b, 1), which, part, tile * P:(tile + 1) * P, :].rearrange("o (h d) t -> d (o h) t", d=DH)).then_inc(s[f"stack{tile}_ld"], 16)

            def v_load(b, tile):
                need_sp("v_st", 16, b, 16)
                need_sp("pv_mm", STEPS, b - 1, HT * 2 * (tile + 1))
                h0 = tile * HT
                sp.dma_start(vst[:, :, h0:h0 + HT, :],
                             v_d[bass.ds(b, 1), :, :, h0:h0 + HT, :].rearrange("o p t h w -> p (o t) (h w)")).then_inc(s[f"v{tile}_ld"], 16)

            def shift(b, g):
                n0, n1 = g * GROUP * TT, (g + 1) * GROUP * TT
                need_sp("shift_c", 5 * (H // GROUP), b, 5 * (g + 1))
                sp.dma_start(shift_d[bass.ds(b, 1), :, n0:n1, :].rearrange("o n m t -> m (o n) t"), shift3[:, :, :]).then_inc(s["shift_st"], 16)
                need_sp("shift_st", 16 * (H // GROUP), b, 16 * (g + 1))
                need_sp("st_mm", 2 * STEPS, b - 1, 4 * GROUP * (g + 1))
                sp.dma_start(qst[KROWS:KROWS + NPART, g * GROUP:(g + 1) * GROUP, :],
                             shift_d[bass.ds(b, 1), :, n0:n1, :].rearrange("o n (h j) t -> (o n) h (j t)", h=GROUP)).then_inc(s["shift_ld"], 16)

            def store_parts(b, j):
                need_sp("qk_l", 2 * KD, b, j + 1)
                sp.dma_start(parts_d[bass.ds(b, 1), j % 2, :, (j // 2) * P:(j // 2 + 1) * P, :].rearrange("o n p t -> p (o n) t"),
                             qk3[:, j % 2, :, :]).then_inc(s[f"parts{j % 2}_st"], 16)

            def store_x2(b):
                need_sp("x2_", 2, b, 2)
                sp.dma_start(rows_of(x2_d, b), x1[:, :, :]).then_inc(s["x2_st"], 16)

            def iteration(i, prev, here, prep):
                last, nxt = i - 1, i + 1
                if not here and prev:
                    sp.wait_ge(s["st_mm"], 2 * STEPS * B)
                    sp.dma_start(raw_down.rearrange("p (r i) -> p r i", i=F), w["down_w"].rearrange("(r p) i -> p r i", p=P)).then_inc(s["raw_down_load"], 16)
                    sp.dma_start(raw_up, w["up_w"].rearrange("(r p) i -> p r i", p=P)).then_inc(s["raw_up_load"], 16)
                if prep:
                    need_sp("sq1", TT, nxt, 0)
                    need_sp("xn1", TT, nxt, 0)
                    sp.dma_start(xa[:, :, :], rows_of(x, nxt)).then_inc(s["xa_load"], 16)
                if not isinstance(i, int) or i >= 2:
                    store_x2(i - 2)
                if prev:
                    need_sp("x1_", 2, last, 0)
                    sp.dma_start(xr[:, :, :], rows_of(x, last)).then_inc(s["xr_load"], 16)
                    need_sp("yt", 2, last, 0)
                    need_sp("x1b", 1, last, 0)
                    sp.dma_start(al[:, :], alpha_d[bass.ds(last, 1), :].broadcast_to([P, 3 * D])).then_inc(s["al_load"], 16)
                if here:
                    v_load(i, 1)
                    shift(i, 1)
                if prep:
                    store_parts(nxt, 0)
                    store_parts(nxt, 1)
                if here:
                    shift(i, 2)
                if prep:
                    store_parts(nxt, 2)
                    store_parts(nxt, 3)
                    if isinstance(i, int) and i == -1:
                        sp.wait_ge(s["wt_hi"], len(WG))
                        sp.wait_ge(s["wt_lo"], len(WG))
                    stack(nxt, 0)
                    need_sp("v_l", TT // 2, nxt, TT // 2)
                    sp.dma_start(v_d[bass.ds(nxt, 1), :, :, :, :].rearrange("o p t h w -> p (o t h w)"), v3[:, :, :, :]).then_inc(s["v_st"], 16)
                    v_load(nxt, 0)
                if here:
                    shift(i, 3)
                if prep:
                    shift(nxt, 0)
                    stack(nxt, 1)
                if prev and not here:
                    store_x2(last)

            run_pipeline(sp, iteration)

            sp.wait_ge(s["x2_st"], 16 * B)

            def tile_of(t, b, n):
                return t[bass.ds(b, 1), n * P:(n + 1) * P, :].rearrange("o p d -> p (o d)")

            def iteration_b(i, *there):
                at = tiles_at(i, *there)
                for z in range(TT):
                    for b, t in at(z, L_SQ3):
                        need_sp("xn3", TT, b, t + 1 - TT)
                        sp.dma_start(xa[:, t, :], tile_of(x2_d, b, t)).then_inc(s[f"x2_ld{t}"], 16)
                    for b, t in at(z, L_DOWN):
                        need_sp("final", TT, b, t + 1)
                        sp.dma_start(tile_of(out, b, t), x1[:, t, :]).then_inc(s[f"out_st{t}"], 16)
                    for b, t in at(z, 0):
                        need_sp("final", TT, b, t + 1 - TT)
                        sp.dma_start(xr[:, t, :], tile_of(x2_d, b, t)).then_inc(s[f"xr_ld{t}"], 16)

            run_pipeline(sp, iteration_b)
            for t in range(TT):
                sp.wait_ge(s[f"out_st{t}"], 16 * B)

        @block.gpsimd
        def _(pool):
            pool.memset(ident[:, :], 0.0).then_inc(s["ident_set"], 1)
            pool.memset(ident_bf[:, :], 0.0).then_inc(s["ident_set"], 1)
            pool.wait_ge(s["ident_set"], 2)
            for m in (ident, ident_bf):
                pool.affine_select(out=m[:, :], in_=m[:, :], compare_op=ALU.not_equal, fill=1.0, base=0,
                                   pattern=[[-1, P]], channel_multiplier=1).then_inc(s["ident_set"], 1)
            pool.memset(ones[:, :], 1.0).then_inc(s["consts_set"], 1)
            pool.memset(half_pow[:, :], -0.5).then_inc(s["consts_set"], 1)
            pool.memset(v3[:, :, :, VW - 1:VW], 1.0).then_inc(s["consts_set"], 1)
            pool.wait_ge(s["consts_set"], 3)

            def rstd(b, i):
                need(pool, f"sq{i}", TT, b, TT)
                past(pool, b)
                st = stat[:, i % 2]
                pool.tensor_scalar(st[:, 1, :], st[:, 0, :], 1.0 / D, EPS, ALU.mult, ALU.add).then_inc(s[f"ms{i}"], 1)
                need(pool, f"ms{i}", 1, b, 1)
                pool.tensor_tensor(st[:, 2, :], st[:, 1, :], half_pow[:, :], ALU.pow).then_inc(s[f"rs{i}"], 1)

            def h_lo(b, i, h):
                for k in range(KD):
                    need(pool, f"hh{i}", KD, b, k + 1)
                    pool.tensor_tensor(h[1][:, k, :], h32[:, k, :], h[0][:, k, :].bitcast(F32), ALU.subtract).then_inc(s[f"hl{i}"], 1)

            def low(b, m):
                need(pool, "ph_", STEPS, b, m + 1)
                need(pool, "pv_mm", STEPS, b, m + 1 - NP_BUF)
                pool.tensor_tensor(pl[:, m % NP_BUF, :], p32[:, m % NP_BUF, :], ph[:, m % NP_BUF, :], ALU.subtract).then_inc(s["pl_pool"], 1)

            def qk_parts(b, j):
                need(pool, "qk_m", 2 * KD, b, j + 1)
                pool.tensor_tensor(qk3[:, j % 2, 2, :], rest[j], qk3[:, j % 2, 1, :], ALU.subtract).then_inc(s["qk_l"], 1)

            def v_parts(b, j):
                need(pool, "v_m", TT // 2, b, j + 1)
                res = rest[2 + j].rearrange("p (t h d) -> p t h d", t=2, h=H)
                pool.tensor_tensor(v3[:, 2 * j:2 * j + 2, :, 2 * DH:3 * DH], res, v3[:, 2 * j:2 * j + 2, :, DH:2 * DH], ALU.subtract).then_inc(s["v_l"], 1)

            def bias(b):
                need(pool, "xn2", TT, b, TT)
                need(pool, "al_load", 16, b, 16)
                pool.tensor_tensor(x1[:, :, :], x1[:, :, :], al[:, 2 * D:3 * D].unsqueeze(1).broadcast_to([P, TT, D]), ALU.add).then_inc(s["x1b"], 1)

            def a_low(b, n):
                need(pool, "ah", NCH, b, n + 1)
                need(pool, "y_mm", NCH, b, n - 1)
                pool.tensor_tensor(a2[1][:, n % 2, :], a32[:, n % 2, :], a2[0][:, n % 2, :].bitcast(F32), ALU.subtract).then_inc(s["a_lo"], 1)

            def iteration(i, *there):
                at, stream = timeline(i, *there)
                for z in range(STEPS):
                    for b in at(z, T_SQ1):
                        rstd(b, 1)
                    for b in at(z, T_SQ2):
                        rstd(b, 2)
                    for n, t in enumerate(T_GH):
                        for b in at(z, t + 1):
                            a_low(b, n)
                    for b in at(z, T_HL1):
                        h_lo(b, 1, hp)
                    for b in at(z, T_HL2):
                        h_lo(b, 2, hs)
                    for j, t in enumerate(T_QK):
                        for b in at(z, t + 2):
                            qk_parts(b, j)
                    for j, t in enumerate(T_V):
                        for b in at(z, t + 2):
                            v_parts(b, j)
                    for b, m in stream(z, T_ST + 1):
                        if m not in ON_DVE:
                            low(b, m)
                    if isinstance(i, int) and i == -1 and z == T_V[1] + 3:
                        pool.wait_ge(s["wt_lo"], len(WG))
                        pool.wait_ge(s["v_l"], TT // 2)
                        pool.memset(kst[KROWS:KROWS + NPART, :, :], 1.0).then_inc(s["kones"], 1)
                        pool.wait_ge(s["kones"], 1)
                    for b in at(z, T_BIAS):
                        bias(b)

            run_pipeline(pool, iteration)

            def rstd_b(b, t):
                need(pool, "sq3", TT, b, t + 1)
                past(pool, b)
                pool.tensor_scalar(stat[:, 0, 1, t:t + 1], stat[:, 0, 0, t:t + 1], 1.0 / D, EPS, ALU.mult, ALU.add).then_inc(s["ms3"], 1)
                need(pool, "ms3", TT, b, t + 1)
                pool.tensor_tensor(stat[:, 0, 2, t:t + 1], stat[:, 0, 1, t:t + 1], half_pow[:, 0:1], ALU.pow).then_inc(s["rs3"], 1)

            def h_lo_b(b, t):
                need(pool, "hh3", TT, b, t + 1)
                a = slice(t * P, (t + 1) * P)
                pool.tensor_tensor(hs[1][:, :, a], h32[:, :, a], hs[0][:, :, a].bitcast(F32), ALU.subtract).then_inc(s["hl3"], 1)

            def integers(b, t):
                need(pool, "q32_", TT, b, t + 1)
                need(pool, "q_t", TT, b, t - 1)
                past(pool, b)
                pool.tensor_scalar(qi[t % 2], q32[t % 2], -ROUND, 1.0, ALU.add, ALU.mult).then_inc(s["qi_"], 1)

            def iteration_b(i, *there):
                at = tiles_at(i, *there)
                for z in range(TT):
                    for b, t in at(z, L_SQ3):
                        rstd_b(b, t)
                    for b, t in at(z, L_HH3):
                        h_lo_b(b, t)
                    for b, t in at(z, L_Q):
                        integers(b, t)

            run_pipeline(pool, iteration_b)

        @block.scalar
        def _(act):
            def split_hi(gs, t_sem, hi_sem, lo_sem):
                for g, (_, dst) in enumerate(gs):
                    act.wait_ge(s[t_sem], g + 1)
                    act.copy(dst[0], wbank[g % 4][:, :]).then_inc(s[hi_sem], 1)

            split_hi(WG, "wt_t", "wt_hi", "wt_lo")

            def squares(b, i, src):
                for t in range(TT):
                    act.activation(xn[:, t, :], src[:, t, :], ACT.Square, accum_out=stat[:, i % 2, 0, t:t + 1]).then_inc(s[f"sq{i}"], 1)

            def h_hi(b, i, h):
                for k in range(KD):
                    need(act, f"h32_{i}", KD, b, k + 1)
                    act.copy(h[0][:, k, :], h32[:, k, :]).then_inc(s[f"hh{i}"], 1)

            def exp(b, m):
                for k in range(2):
                    need(act, "st_mm", 2 * STEPS, b, 2 * m + k + 1)
                    if k == 0:
                        need_low(act, b, m - NP_BUF)
                    act.activation(p32[:, m % NP_BUF, k * S:(k + 1) * S], stb[k], ACT.Exp, scale=SCALE).then_inc(s["exp_"], 1)

            def high(b, m):
                need(act, "exp_", 2 * STEPS, b, 2 * m + 2)
                need(act, "pv_mm", STEPS, b, m + 1 - NP_BUF)
                act.copy(ph[:, m % NP_BUF, :], p32[:, m % NP_BUF, :]).then_inc(s["ph_"], 1)

            def tanh(b, n):
                need(act, "gh_mm", NCH, b, n + 1)
                if n == 0:
                    need(act, "qk_l", 2 * KD, b + 2, 2)
                need(act, "u_", NCH, b, n - 1)
                act.activation(th[:, n % 2, :], gen[n % 2][:, 0:HALF], ACT.Tanh, scale=0.5).then_inc(s["tanh_"], 1)

            def a_high(b, n):
                need(act, "a_", NCH, b, n + 1)
                need(act, "y_mm", NCH, b, n - 1)
                act.copy(a2[0][:, n % 2, :], a32[:, n % 2, :]).then_inc(s["ah"], 1)

            def qk_high(b, j):
                need(act, "qk_mm", 2 * KD, b, j + 1)
                need(act, f"parts{j % 2}_st", 16 * KD, b, 16 * (j // 2))
                act.copy(qk3[:, j % 2, 0, :], gen[QK_BANK[j]][:, :]).then_inc(s["qk_h"], 1)

            def v_high(b, j):
                need(act, "v_mm", TT // 2, b, j + 1)
                need(act, "v_st", 16, b, 0)
                act.copy(v3[:, 2 * j:2 * j + 2, :, 0:DH], gen[V_BANK[j]][:, :].rearrange("p (t h d) -> p t h d", t=2, h=H)).then_inc(s["v_h"], 1)

            def qk_middle(b, j):
                need(act, "qk_r", 2 * KD, b, j + 1)
                act.copy(qk3[:, j % 2, 1, :], rest[j]).then_inc(s["qk_m"], 1)

            def v_middle(b, j):
                need(act, "v_r", TT // 2, b, j + 1)
                act.copy(v3[:, 2 * j:2 * j + 2, :, DH:2 * DH], rest[2 + j].rearrange("p (t h d) -> p t h d", t=2, h=H)).then_inc(s["v_m"], 1)

            def o_high(b):
                need(act, "gh_mm", NCH, b, 0)
                for k in range(KD):
                    need(act, "o_t", KD, b, k + 1)
                    act.copy(hs[0][:, k, :], gen[OT_BANK[k]][:, :]).then_inc(s["oh"], 1)

            def iteration(i, *there):
                at, stream = timeline(i, *there)
                for z in range(STEPS):
                    for j, t in enumerate(T_QK):
                        for b in at(z, t + 1):
                            qk_high(b, j)
                    for j, t in enumerate(T_V):
                        for b in at(z, t + 1):
                            v_high(b, j)
                    for n, t in enumerate(T_GH):
                        for b in at(z, t + 1):
                            tanh(b, n)
                    for b, m in stream(z, T_ST):
                        exp(b, m)
                    for j, t in enumerate(T_QK):
                        for b in at(z, t + 2):
                            qk_middle(b, j)
                    for j, t in enumerate(T_V):
                        for b in at(z, t + 2):
                            v_middle(b, j)
                    for b in at(z, T_OT + 1):
                        o_high(b)
                    for b in at(z, T_SQ1):
                        need(act, "xa_load", 16, b, 16)
                        need(act, "v_l", TT // 2, b, 0)
                        need(act, "xt2", KD, b - 3, KD)
                        squares(b, 1, xa)
                    for b in at(z, T_HH1):
                        need(act, "v_mm", TT // 2, b, 0)
                        h_hi(b, 1, hp)
                    for b in at(z, T_SQ2):
                        need(act, "x1_", 2, b, 2)
                        need(act, "xt1", KD, b + 2, KD)
                        squares(b, 2, x1)
                    for b in at(z, T_HH2):
                        h_hi(b, 2, hs)
                    for n, t in enumerate(T_GH):
                        for b in at(z, t + 1):
                            a_high(b, n)
                    for b, m in stream(z, T_ST + 1):
                        high(b, m)

            run_pipeline(act, iteration)

            split_hi(WG_UP, "up_t", "up_hi", "up_lo")

            def iteration_b(i, *there):
                at = tiles_at(i, *there)
                for z in range(TT):
                    for b, t in at(z, L_HH3):
                        need(act, "h32_3", KD * TT, b, KD * (t + 1))
                        need(act, "v2_mm", 2 * TT, b, 2 * (t + 1 - TT))
                        a = slice(t * P, (t + 1) * P)
                        act.copy(hs[0][:, :, a], h32[:, :, a]).then_inc(s["hh3"], 1)
                    for b, t in at(z, L_SQ3):
                        need(act, f"x2_ld{t}", 16, b, 16)
                        need(act, "xt3", TT, b, t + 1 - TT)
                        act.activation(xn[:, t, :], xa[:, t, :], ACT.Square, accum_out=stat[:, 0, 0, t:t + 1]).then_inc(s["sq3"], 1)
                    for b, t in at(z, 0):
                        for c in range(2):
                            need(act, "g_mm", 2 * TT, b, 2 * t + c + 1)
                            need(act, "hmul", 2 * TT, b, 2 * t + c - 1)
                            act.activation(ge[:, c, 0:S], smb[c], ACT.Gelu).then_inc(s["gelu"], 1)

            run_pipeline(act, iteration_b)

        @block.vector
        def _(dve):
            dve.wait_ge(s["cond_t"], 1)
            dve.tensor_copy(condT[:, :], gen[0][0:C, 0:B]).then_inc(s["cond_tc"], 1)
            dve.wait_ge(s["cw_t"], 1)
            n_cwT = len(KINDS) * D
            dve.tensor_copy(p32_flat[0:C, n_cw:n_cw + n_cwT], core_flat[0:C, 0:n_cwT]).then_inc(s["cw_tc"], 1)
            dve.wait_ge(s["tab_mm"], 1)
            nt = NSC * KD
            dve.tensor_copy(table[:, 0:nt - KD, :].rearrange("p n b -> p (n b)"), gen[1][:, 0:(nt - KD) * B]).then_inc(s["tab_copy"], 1)
            dve.tensor_scalar(table[:, nt - KD:nt, :].rearrange("p n b -> p (n b)"), gen[1][:, (nt - KD) * B:nt * B], 1.0, None, ALU.add).then_inc(s["tab_copy"], 1)
            dve.wait_ge(s["row_mm"], 1)
            dve.tensor_copy(arow[:, 0:2 * D], pvb[0:B, :]).then_inc(s["row_copy"], 1)
            dve.wait_ge(s["row_copy"], 1)
            dve.wait_ge(s["ob_load"], 16)
            dve.tensor_tensor(arow[:, 2 * D:3 * D], arow[:, D:2 * D], obrow[:, :], ALU.mult).then_inc(s["row_ob"], 1)

            def split_lo(gs, hi_sem, lo_sem):
                for g, (_, dst) in enumerate(gs):
                    dve.wait_ge(s[hi_sem], g + 1)
                    dve.tensor_tensor(dst[1], wbank[g % 4][:, :], dst[0].bitcast(F32), ALU.subtract).then_inc(s[lo_sem], 1)

            split_lo(WG, "wt_hi", "wt_lo")
            dve.wait_ge(s["tab_copy"], 2)

            def xnorm(b, i, src):
                need(dve, f"rs{i}", 1, b, 1)
                for t in range(TT):
                    dve.tensor_scalar(xn[:, t, :], src[:, t, :], stat[:, i % 2, 2, t:t + 1], None, ALU.mult).then_inc(s[f"xn{i}"], 1)

            def affine(b, i, gamma, beta, c):
                for k in range(KD):
                    need(dve, f"xt{i}", KD, b, k + 1)
                    scale = cur[:, c, gamma * KD + k:gamma * KD + k + 1]
                    if beta is None:
                        dve.tensor_scalar(h32[:, k, :], gen[XT_BANK[k]][:, :], scale, None, ALU.mult).then_inc(s[f"h32_{i}"], 1)
                    else:
                        dve.tensor_scalar(h32[:, k, :], gen[XT_BANK[k]][:, :], scale, cur[:, c, beta * KD + k:beta * KD + k + 1],
                                          ALU.mult, ALU.add).then_inc(s[f"h32_{i}"], 1)

            def tiles(t):
                return t.rearrange("p (t d) -> p t d", t=2)

            def scaled(name, to, src, col):
                dve.tensor_tensor(tiles(to), tiles(src[:, :]),
                                  al[:, col:col + D].unsqueeze(1).broadcast_to([P, 2, D]), ALU.mult).then_inc(s[name], 1)

            def maxima(b, n):
                need(dve, "smax_mm", 2 * STEPS, b, n + 1)
                dve.tensor_reduce(negmax[:, n // TT, n % TT:n % TT + 1], smb[n % 2], AX_X, ALU.max, negate=True).then_inc(s["smax"], 1)

            def shift_parts(b, g):
                ng = H // GROUP
                need(dve, "shift_t", ng, b, g + 1)
                dve.tensor_scalar(shift32[:, 0, :], smb[0][0:GROUP * TT, 0:P], P_SHIFT / SCALE, None, ALU.add).then_inc(s["shift_c"], 1)
                need(dve, "shift_st", 16 * ng, b, 16 * g)
                need(dve, "shift_c", 5 * ng, b, 5 * g + 1)
                dve.tensor_copy(shift3[:, 0, :], shift32[:, 0, :]).then_inc(s["shift_c"], 1)
                need(dve, "shift_c", 5 * ng, b, 5 * g + 2)
                dve.tensor_tensor(shift32[:, 1, :], shift32[:, 0, :], shift3[:, 0, :], ALU.subtract).then_inc(s["shift_c"], 1)
                need(dve, "shift_c", 5 * ng, b, 5 * g + 3)
                dve.tensor_copy(shift3[:, 1, :], shift32[:, 1, :]).then_inc(s["shift_c"], 1)
                need(dve, "shift_c", 5 * ng, b, 5 * g + 4)
                dve.tensor_tensor(shift3[:, 2, :], shift32[:, 1, :], shift3[:, 1, :], ALU.subtract).then_inc(s["shift_c"], 1)

            def low(b, m):
                need(dve, "ph_", STEPS, b, m + 1)
                need(dve, "pv_mm", STEPS, b, m + 1 - NP_BUF)
                dve.tensor_tensor(pl[:, m % NP_BUF, :], p32[:, m % NP_BUF, :], ph[:, m % NP_BUF, :], ALU.subtract).then_inc(s["pl_dve"], 1)

            def heads_out(b, r):
                need(dve, "pv_mm", STEPS, b, 4 * r + 4)
                need(dve, "o_norm", H, b, 2 * r)
                pv = pvb[:, 0:2 * TT * VW].rearrange("p (q w) -> p q w", w=VW)
                dve.tensor_reduce(osum[:, :, :], pv[:, :, 0:NPART * DH].rearrange("p q (n d) -> p q d n", n=NPART),
                                  AX_X, ALU.add).then_inc(s["o_sum"], 1)
                dve.reciprocal(orec[:, :].unsqueeze(2), pv[:, :, VW - 1:VW]).then_inc(s["o_rec"], 1)
                need(dve, "o_sum", H // 2, b, r + 1)
                need(dve, "o_rec", H // 2, b, r + 1)
                if r == 0:
                    need(dve, "o_t", KD, b, 0)
                for k in range(2):
                    h = 2 * r + k
                    dve.tensor_tensor(o[:, :, h * DH:(h + 1) * DH], osum[:, k * TT:(k + 1) * TT, :],
                                      orec[:, k * TT:(k + 1) * TT].unsqueeze(2).broadcast_to([P, TT, DH]), ALU.mult).then_inc(s["o_norm"], 1)

            def qk_rest(b, j):
                need(dve, "qk_h", 2 * KD, b, j + 1)
                dve.tensor_tensor(rest[j], gen[QK_BANK[j]][:, :], qk3[:, j % 2, 0, :], ALU.subtract).then_inc(s["qk_r"], 1)

            def v_rest(b, j):
                need(dve, "v_h", TT // 2, b, j + 1)
                need(dve, "qk_l", 2 * KD, b, 3 + j)
                dve.tensor_tensor(rest[2 + j].rearrange("p (t h d) -> p t h d", t=2, h=H),
                                  gen[V_BANK[j]][:, :].rearrange("p (t h d) -> p t h d", t=2, h=H),
                                  v3[:, 2 * j:2 * j + 2, :, 0:DH], ALU.subtract).then_inc(s["v_r"], 1)

            def o_low(b):
                for k in range(KD):
                    need(dve, "oh", KD, b, k + 1)
                    dve.tensor_tensor(hs[1][:, k, :], gen[OT_BANK[k]][:, :], hs[0][:, k, :].bitcast(F32), ALU.subtract).then_inc(s["ol"], 1)

            def first_residual(b, c):
                if c == 0:
                    need(dve, "al_load", 16, b, 16)
                    need(dve, "xr_load", 16, b, 16)
                    need(dve, "x2_st", 16, b, 0)
                    need(dve, "qk_l", 2 * KD, b + 1, 2 * KD)
                need(dve, "oproj", 2, b, c + 1)
                scaled("xt_", xt[c], gen[OP_BANK[c]], 0)
                need(dve, "xt_", 2, b, c + 1)
                dve.tensor_tensor(x1[:, 2 * c:2 * c + 2, :], tiles(xt[c]), xr[:, 2 * c:2 * c + 2, :], ALU.add).then_inc(s["x1_"], 1)

            def swiglu(b, n):
                need(dve, "tanh_", NCH, b, n + 1)
                dve.scalar_tensor_tensor(out=ug[:, n % 2, :], in0=th[:, n % 2, :], scalar=1.0,
                                         in1=gen[n % 2][:, 0:HALF], op0=ALU.add, op1=ALU.mult).then_inc(s["u_"], 1)
                need(dve, "u_", NCH, b, n + 1)
                need(dve, "a_lo", NCH, b, n - 1)
                dve.scalar_tensor_tensor(out=a32[:, n % 2, :], in0=ug[:, n % 2, :], scalar=0.5,
                                         in1=gen[n % 2][:, HALF:2 * HALF], op0=ALU.mult, op1=ALU.mult).then_inc(s["a_"], 1)

            def second_residual(b, c):
                if c == 0:
                    need(dve, "x1b", 1, b, 1)
                need(dve, "y_mm", NCH, b, KF * (c + 1))
                scaled("yt", h32[:, c, :], gen[Y_BANK], D)
                need(dve, "yt", 2, b, c + 1)
                dve.tensor_tensor(x1[:, 2 * c:2 * c + 2, :], tiles(h32[:, c, :]), x1[:, 2 * c:2 * c + 2, :], ALU.add).then_inc(s["x2_"], 1)

            def ternary_weights():
                dve.wait_ge(s["raw_down_load"], 16)
                dve.tensor_reduce(wabs[:, :], raw_down, AX_X, ALU.add, apply_absolute_value=True).then_inc(s["wsum"], 1)
                dve.wait_ge(s["wsum_mm"], 1)
                dve.tensor_scalar(wmean[:, :], pvb[:, 0:1], 1.0 / (D * F), QUANT_EPS, ALU.mult, ALU.max).then_inc(s["wq_"], 1)
                dve.wait_ge(s["wq_"], 1)
                dve.reciprocal(winv[:, :], wmean[:, :]).then_inc(s["wq_"], 1)
                dve.wait_ge(s["wq_"], 2)
                dve.tensor_scalar(tern_t, raw_down, winv[:, 0:1], 1.0, ALU.mult, ALU.min).then_inc(s["wq_"], 1)
                dve.wait_ge(s["wq_"], 3)
                dve.tensor_scalar(raw_down, tern_t, -1.0, ROUND, ALU.max, ALU.add).then_inc(s["wq_"], 1)
                dve.wait_ge(s["wq_"], 4)
                dve.tensor_scalar(tern, raw_down, ROUND, None, ALU.subtract).then_inc(s["tern"], 1)
                dve.wait_ge(s["tern_t_"], 1)
                dve.tensor_copy(wdown[:, :, :].rearrange("p k n -> p (k n)"), core_flat[:, 0:KD * P * KF // 2].bitcast(BF16)).then_inc(s["tern_c"], 1)

            def iteration(i, *there):
                at, stream = timeline(i, *there)
                for z in range(STEPS):
                    for c in range(2):
                        for b in at(z, T_DOWN[KF * (c + 1) - 1] + 1):
                            second_residual(b, c)
                    for b, m in stream(z, T_PV + 1):
                        if m % 4 == 3:
                            heads_out(b, m // 4)
                    for g, t in enumerate(T_TURN):
                        for b in at(z, t):
                            shift_parts(b, g)
                    if isinstance(i, int) and i == B and z == Z_TERN:
                        ternary_weights()
                    for b, m in stream(z, T_MAX):
                        maxima(b, 2 * m)
                    for n, t in enumerate(T_GH):
                        for b in at(z, t + 1):
                            swiglu(b, n)
                    for b, m in stream(z, T_MAX):
                        maxima(b, 2 * m + 1)
                    for b in at(z, T_XN1):
                        dve.tensor_copy(cur[:, 0, :].unsqueeze(2), table[:, :, bass.ds(b, 1)]).then_inc(s["cur_set"], 1)
                        xnorm(b, 1, xa)
                    for b in at(z, T_H1):
                        need(dve, "cur_set", 1, b, 1)
                        affine(b, 1, 0, 1, 0)
                    for c in range(2):
                        for b in at(z, T_OP[c] + 1):
                            first_residual(b, c)
                    for b in at(z, T_XN2):
                        dve.tensor_copy(cur[:, 1, :].unsqueeze(2), table[:, :, bass.ds(b, 1)]).then_inc(s["cur2_set"], 1)
                        xnorm(b, 2, x1)
                    for b in at(z, T_H2):
                        need(dve, "cur2_set", 1, b, 1)
                        need(dve, "hl1", KD, b + 2, KD)
                        affine(b, 2, 2, 3, 1)
                    for b, m in stream(z, T_ST + 1):
                        if m in ON_DVE:
                            low(b, m)
                    for b in at(z, T_OT + 1):
                        o_low(b)
                    for j, t in enumerate(T_QK):
                        for b in at(z, t + 1):
                            qk_rest(b, j)
                    for j, t in enumerate(T_V):
                        for b in at(z, t + 1):
                            v_rest(b, j)

            run_pipeline(dve, iteration)

            split_lo(WG_UP, "up_hi", "up_lo")

            def norm_b(b, t):
                if t == 0:
                    need(dve, "h32_3", KD * TT, b, 0)
                    dve.tensor_copy(cur[:, 0, :].unsqueeze(2), table[:, :, bass.ds(b, 1)]).then_inc(s["cur_set"], 1)
                need(dve, "rs3", TT, b, t + 1)
                dve.tensor_scalar(xn[:, t, :], xa[:, t, :], stat[:, 0, 2, t:t + 1], None, ALU.mult).then_inc(s["xn3"], 1)

            def scale_b(b, t):
                need(dve, "xt3", TT, b, t + 1)
                if t == 0:
                    need(dve, "cur_set", 1, b, B + 1)
                for k in range(KD):
                    dve.tensor_scalar(h32[:, k, t * P:(t + 1) * P], xt_bank[:, k * P:(k + 1) * P], cur[:, 0, 4 * KD + k:4 * KD + k + 1],
                                      None, ALU.mult).then_inc(s["h32_3"], 1)

            def h_mul(b, t, c):
                need(dve, "gelu", 2 * TT, b, 2 * t + c + 1)
                need(dve, "v2_mm", 2 * TT, b, 2 * t + c + 1)
                dve.tensor_tensor(hb[t % 2][:, c * S:(c + 1) * S], stb[c], ge[:, c, 0:S], ALU.mult).then_inc(s["hmul"], 1)

            def quantise(b, t):
                need(dve, "hmul", 2 * TT, b, 2 * t + 2)
                q = [qs[:, t, n:n + 1] for n in range(4)]
                dve.tensor_reduce(q[0], hb[t % 2], AX_X, ALU.max, apply_absolute_value=True).then_inc(s["amax"], 1)
                need(dve, "amax", TT, b, t + 1)
                dve.tensor_scalar(q[1], q[0], QUANT_EPS, 1.0 / 127.0, ALU.max, ALU.mult).then_inc(s["qscale"], 1)
                need(dve, "qscale", 3 * TT, b, 3 * t + 1)
                dve.reciprocal(q[2], q[1]).then_inc(s["qscale"], 1)
                dve.tensor_scalar(q[3], q[1], wmean[:, 0:1], None, ALU.mult).then_inc(s["qscale"], 1)
                need(dve, "qscale", 3 * TT, b, 3 * t + 3)
                need(dve, "qi_", TT, b, t - 1)
                dve.tensor_scalar(q32[t % 2], hb[t % 2], q[2], ROUND, ALU.mult, ALU.add).then_inc(s["q32_"], 1)

            def q_copy(b, t):
                need(dve, "q_t", TT, b, t + 1)
                need(dve, "d_mm", TT, b, t - 1)
                dve.tensor_scalar(qT[t % 2], qt_bank, 127.0, -128.0, ALU.min, ALU.max).then_inc(s["q_tc"], 1)

            def finish(b, t):
                need(dve, "d_mm", TT, b, t + 1)
                need(dve, f"xr_ld{t}", 16, b, 16)
                need(dve, f"out_st{t}", 16, b, 0)
                dve.scalar_tensor_tensor(out=x1[:, t, :], in0=down_bank, scalar=qs[:, t, 3:4],
                                         in1=xr[:, t, :], op0=ALU.mult, op1=ALU.add).then_inc(s["final"], 1)

            def iteration_b(i, *there):
                at = tiles_at(i, *there)
                for z in range(TT):
                    for b, t in at(z, L_H3):
                        scale_b(b, t)
                    for b, t in at(z, L_XN3):
                        norm_b(b, t)
                    for b, t in at(z, 0):
                        h_mul(b, t, 0)
                    for b, t in at(z, L_DOWN):
                        finish(b, t)
                    for b, t in at(z, 0):
                        h_mul(b, t, 1)
                    for b, t in at(z, L_QT):
                        q_copy(b, t)
                    for b, t in at(z, 0):
                        quantise(b, t)

            run_pipeline(dve, iteration_b)

        @block.tensor
        def _(pe):
            def exact(out_, terms, start=True, stop=True, **kw):
                passes = [(l[a], r[c]) for l, r in terms for a, c in ((0, 0), (0, 1), (1, 0))]
                for i, (l, r) in enumerate(passes):
                    last = pe.matmul(out_, l, r, start=start and i == 0, stop=stop and i == len(passes) - 1, **kw)
                return last

            pe.wait_ge(s["ident_set"], 4)
            pe.wait_ge(s["cond_load"], 16 * (1 + len(KINDS)))
            pe.transpose(gen[0][0:C, 0:B], condr[:, :], ident[0:B, 0:B]).then_inc(s["cond_t"], 1)
            for i in range(len(KINDS)):
                for k in range(KD):
                    last = pe.transpose(core_flat[0:C, (i * KD + k) * P:(i * KD + k + 1) * P], cw[:, i, k, :], ident[:, :])
            last.then_inc(s["cw_t"], 1)
            pe.wait_ge(s["cond_tc"], 1)
            pe.wait_ge(s["cw_tc"], 1)
            for i in range(NSC):
                for k in range(KD):
                    n = i * KD + k
                    last = pe.matmul(gen[1][:, n * B:(n + 1) * B], cwT[:, i, k * P:(k + 1) * P], condT[:, :], start=True, stop=True)
            last.then_inc(s["tab_mm"], 1)
            pe.matmul(pvb[0:B, :], condT[:, :], cwT[:, NSC:NSC + 2, :].rearrange("c n d -> c (n d)"), start=True, stop=True).then_inc(s["row_mm"], 1)
            pe.wait_ge(s["tab_copy"], 2)
            pe.wait_ge(s["row_copy"], 1)

            def transpose_weights(gs, t_sem, lo_sem):
                for g, (src, _) in enumerate(gs):
                    if gs is WG and g == 4 * KD * KD // 4:
                        pe.wait_ge(s["raw_ffn_load"], 16 * 3)
                    if g >= 4:
                        pe.wait_ge(s[lo_sem], g - 3)
                    for i, a in enumerate(src):
                        last = pe.transpose(wbank[g % 4][:, i * P:(i + 1) * P], a, ident[:, :])
                    last.then_inc(s[t_sem], 1)

            pe.wait_ge(s["raw_qkvo_load"], 16 * 4)
            transpose_weights(WG, "wt_t", "wt_lo")
            pe.wait_ge(s["wt_lo"], len(WG))
            pe.wait_ge(s["consts_set"], 3)

            def norm_t(b, i):
                need(pe, f"xn{i}", TT, b, TT)
                for k in range(KD):
                    for t in range(TT):
                        last = pe.transpose(gen[XT_BANK[k]][:, t * P:(t + 1) * P], xn[:, t, k * P:(k + 1) * P], ident[:, :])
                    last.then_inc(s[f"xt{i}"], 1)

            def col(pair, k, a, n):
                return [t[:, k, a:a + n] for t in pair]

            def scores_max(b, n):
                if n % (2 * TT * HT // 2) == 0:
                    tile = n // (TT * HT)
                    need(pe, f"stack{tile}_ld", 192, b, 192)
                need(pe, "smax", 2 * STEPS, b, n - 1)
                h, q = n // TT, n % TT
                pe.matmul(smb[n % 2], qst[0:KROWS, h, q * P:(q + 1) * P], kst[0:KROWS, h, :], start=True, stop=True).then_inc(s["smax_mm"], 1)

            def shift_turn(b, g):
                need(pe, "smax", 2 * STEPS, b, TT * GROUP * (g + 1))
                pe.transpose(smb[0][0:GROUP * TT, 0:P], negmax[:, g * GROUP:(g + 1) * GROUP, :].rearrange("p h t -> p (h t)"), ident[:, :]).then_inc(s["shift_t"], 1)

            def scores(b, m):
                h = m // 2
                if m % (2 * GROUP) == 0:
                    need(pe, "shift_ld", 16 * (H // GROUP), b, 16 * (m // (2 * GROUP) + 1))
                for k in range(2):
                    need(pe, "exp_", 2 * STEPS, b, 2 * m + k - 1)
                    k0 = (2 * (m % 2) + k) * P
                    last = pe.matmul(stb[k], kst[0:KROWS + NPART, h, k0:k0 + P], qst[0:KROWS + NPART, h, :], start=True, stop=True)
                    last.then_inc(s["st_mm"], 1)

            def weighted(b, m):
                h = m // 2
                if m % (2 * HT) == 0:
                    need(pe, f"v{m // (2 * HT)}_ld", 16, b, 16)
                if m % 4 == 0:
                    need(pe, "o_rec", H // 2, b, h // 2)
                need(pe, "ph_", STEPS, b, m + 1)
                need_low(pe, b, m)
                for q in range(TT):
                    for k in range(2):
                        for part in (ph, pl):
                            a, w0 = k * S + q * P, ((h % 2) * TT + q) * VW
                            last = pe.matmul(pvb[:, w0:w0 + VW], part[:, m % NP_BUF, a:a + P], vst[:, 2 * (m % 2) + k, h, :],
                                             start=(m % 4 == 0 and q == 0 and k == 0 and part is ph),
                                             stop=(m % 2 == 1 and k == 1 and part is pl), skip_group_check=True)
                last.then_inc(s["pv_mm"], 1)

            def project_qk(b, j):
                if j == 0:
                    need(pe, "hl1", KD, b, KD)
                for name, per, other, k in ((), (("xt_", 2, b - 2, 1),), (("qk_r", 2 * KD, b, 2),), (("h32_2", KD, b - 2, 1), ("xt_", 2, b - 2, 2)))[j]:
                    need(pe, name, per, other, k)
                col0 = ((j % 2) * KD + j // 2) * P
                exact(gen[QK_BANK[j]][:, :], [(col(wqkv, k, col0, P), col(hp, k, 0, S)) for k in range(KD)]).then_inc(s["qk_mm"], 1)

            def project_v(b, j):
                if j == 0:
                    need(pe, "h32_2", KD, b - 2, 2)
                need(pe, "qk_r", 2 * KD, b, (1, 2 * KD)[j])
                for t in range(2):
                    last = exact(gen[V_BANK[j]][:, t * D:(t + 1) * D],
                                 [(col(hp, k, (2 * j + t) * P, P), col(wqkv, k, 2 * D, D)) for k in range(KD)])
                last.then_inc(s["v_mm"], 1)

            def turn_o(b):
                need(pe, "o_norm", H, b, H)
                need(pe, "a_", NCH, b, 0)
                need(pe, "v_r", TT // 2, b + 1, TT // 2)
                for k in range(KD):
                    for t in range(TT):
                        last = pe.transpose(gen[OT_BANK[k]][:, t * P:(t + 1) * P], o[:, t, k * P:(k + 1) * P], ident[:, :])
                    last.then_inc(s["o_t"], 1)

            def project_o(b, c):
                if c == 0:
                    need(pe, "ol", KD, b, KD)
                if c == 1:
                    need(pe, "yt", 2, b, 0)
                    need(pe, "h32_1", KD, b + 2, 1)
                for t in range(2):
                    last = exact(gen[OP_BANK[c]][:, t * D:(t + 1) * D],
                                 [(col(oT, k, (2 * c + t) * P, P), col(wo, k, 0, D)) for k in range(KD)])
                last.then_inc(s["oproj"], 1)

            def gate_hidden(b, n):
                c, j = n // KF, n % KF
                if n == 0:
                    need(pe, "hl2", KD, b, KD)
                    need(pe, "v_r", TT // 2, b + 2, 1)
                need(pe, "a_", NCH, b, n - 1)
                for k2 in range(2):
                    last = exact(gen[n % 2][:, k2 * HALF:(k2 + 1) * HALF],
                                 [(col(wgh, k, k2 * F + j * P, P), col(hs, k, c * HALF, HALF)) for k in range(KD)])
                last.then_inc(s["gh_mm"], 1)

            def swiglu_down(b, n):
                c, j = n // KF, n % KF
                if n == 0:
                    need(pe, "v_r", TT // 2, b + 2, 2)
                if n == KF:
                    need(pe, "yt", 2, b, 1)
                need(pe, "ah", NCH, b, n + 1)
                need(pe, "a_lo", NCH, b, n + 1)
                for t in range(2):
                    last = exact(gen[Y_BANK][:, t * D:(t + 1) * D],
                                 [([p[:, n % 2, t * P:(t + 1) * P] for p in a2], [p[:, j, :] for p in wout])],
                                 start=(j == 0 and t == 0), stop=(j == KF - 1), skip_group_check=True)
                last.then_inc(s["y_mm"], 1)

            def ternary_weights():
                pe.wait_ge(s["wsum"], 1)
                pe.matmul(pvb[:, 0:1], ones[:, :], wabs[:, :], start=True, stop=True).then_inc(s["wsum_mm"], 1)
                pe.wait_ge(s["tern"], 1)
                down_t = core_flat[:, 0:KD * P * KF // 2].bitcast(BF16)
                for j in range(KF):
                    for r in range(KD):
                        last = pe.transpose(down_t[:, (j * KD + r) * P:(j * KD + r + 1) * P], tern[:, r * F + j * P:r * F + (j + 1) * P], ident_bf[:, :])
                last.then_inc(s["tern_t_"], 1)

            def iteration(i, *there):
                at, stream = timeline(i, *there)
                for z in range(STEPS):
                    if isinstance(i, int) and i == B and z == Z_TERN:
                        ternary_weights()
                    turned = [(b, g) for g, t in enumerate(T_TURN) for b in at(z, t)]
                    for b, g in turned:
                        shift_turn(b, g)
                    if not turned:
                        for b, m in stream(z, T_MAX):
                            scores_max(b, 2 * m)
                    for b, m in stream(z, T_ST):
                        if isinstance(b, int) and b == 0 and m == 0:
                            pe.wait_ge(s["kones"], 1)
                        scores(b, m)
                    for b, m in stream(z, T_PV):
                        weighted(b, m)
                    for b, g in turned:
                        need(pe, "shift_c", 5 * (H // GROUP), b, 5 * g + 1)
                        for b2, m in stream(z, T_MAX):
                            scores_max(b2, 2 * m)
                    for b, m in stream(z, T_MAX):
                        scores_max(b, 2 * m + 1)
                    for b in at(z, T_OT):
                        turn_o(b)
                    for b in at(z, T_XT1):
                        need(pe, "v_r", TT // 2, b, 0)
                        need(pe, "yt", 2, b - 3, 2)
                        need(pe, "ol", KD, b - 2, 1)
                        norm_t(b, 1)
                    for c in range(2):
                        for b in at(z, T_OP[c]):
                            project_o(b, c)
                    for j, t in enumerate(T_QK):
                        for b in at(z, t):
                            project_qk(b, j)
                    for b in at(z, T_XT2):
                        need(pe, "qk_r", 2 * KD, b + 2, 1)
                        norm_t(b, 2)
                    for j, t in enumerate(T_V):
                        for b in at(z, t):
                            project_v(b, j)
                    for n, t in enumerate(T_GH):
                        for b in at(z, t):
                            gate_hidden(b, n)
                    for n, t in enumerate(T_DOWN):
                        for b in at(z, t):
                            swiglu_down(b, n)

            run_pipeline(pe, iteration)

            pe.wait_ge(s["x2_"], 2 * B)
            pe.wait_ge(s["raw_up_load"], 16)
            transpose_weights(WG_UP, "up_t", "up_lo")
            pe.wait_ge(s["up_lo"], len(WG_UP))
            pe.wait_ge(s["tern_c"], 1)

            def norm_t_b(b, t):
                need(pe, "xn3", TT, b, t + 1)
                need(pe, "h32_3", KD * TT, b, KD * t)
                for k in range(KD):
                    last = pe.transpose(xt_bank[:, k * P:(k + 1) * P], xn[:, t, k * P:(k + 1) * P], ident[:, :])
                last.then_inc(s["xt3"], 1)

            def unit(b, t, c):
                if c == 0:
                    need(pe, "hl3", TT, b, t + 1)
                for bank, first, sem_, free in ((smb[c], F, "g_mm", "gelu"), (stb[c], 0, "v2_mm", "hmul")):
                    need(pe, free, 2 * TT, b, 2 * t + c - 1)
                    exact(bank, [(col(hs, k, t * P, P), col(wup, k, first + c * S, S)) for k in range(KD)]).then_inc(s[sem_], 1)

            def q_transpose(b, t):
                need(pe, "qi_", TT, b, t + 1)
                need(pe, "q_tc", TT, b, t)
                for j in range(KF):
                    last = pe.transpose(qt_bank[:, j * P:(j + 1) * P], qi[t % 2][:, j * P:(j + 1) * P], ident_bf[:, :])
                last.then_inc(s["q_t"], 1)

            def down(b, t):
                need(pe, "q_tc", TT, b, t + 1)
                need(pe, "final", TT, b, t)
                for j in range(KF):
                    last = pe.matmul(down_bank, qT[t % 2][:, j * P:(j + 1) * P], wdown[:, j, :], start=(j == 0), stop=(j == KF - 1))
                last.then_inc(s["d_mm"], 1)

            def iteration_b(i, *there):
                at = tiles_at(i, *there)
                for z in range(TT):
                    for b, t in at(z, 0):
                        unit(b, t, 0)
                    for b, t in at(z, L_DOWN):
                        down(b, t)
                    for b, t in at(z, 0):
                        unit(b, t, 1)
                    for b, t in at(z, L_QT):
                        q_transpose(b, t)
                    for b, t in at(z, L_XT3):
                        norm_t_b(b, t)

            run_pipeline(pe, iteration_b)


_L0 = ("attn_gamma_w", "attn_beta_w", "W_q", "W_k", "W_v", "W_o", "attn_alpha_w", "ffn_gamma_w", "ffn_beta_w",
       "gate_w", "hidden_w", "out_w", "out_b", "ffn_alpha_w")
_L1 = ("norm_w", "up_w", "down_w")
_INS = ["x", "cond_256"] + ["L0_cond_" + n for n in _L0] + ["L1_cond_" + n for n in _L1]


def kernel(**inputs):
    import numpy as _np
    import concourse.bacc as _bacc
    from concourse.bass_utils import run_bass_kernel_spmd as _run

    nc = _bacc.Bacc("TRN2", target_bir_lowering=False, num_devices=1)
    arrays, aps = {}, {}
    for name in _INS:
        a = _np.ascontiguousarray(inputs[name])
        arrays[f"in_{name}_dram"] = a
        aps[name] = nc.dram_tensor(f"in_{name}_dram", a.shape, mybir.dt.from_np(a.dtype), kind="ExternalInput").ap()
    out = nc.dram_tensor("out_dram", arrays["in_x_dram"].shape, F32, kind="ExternalOutput").ap()
    w = {n.split("_cond_")[1]: aps[n] for n in _INS[2:]}
    build(nc, aps["x"], aps["cond_256"], w, out)
    r = _run(nc, [arrays], core_ids=[0])
    return r.results[0]["out_dram"]
```
